# Optimizing a Trainium2 kernel written in Bass

```python
import numpy as np
import jax
import jax.numpy as jnp

def _softmax(x, axis=-1):
    return jax.nn.softmax(x, axis=axis)

def _gelu(x):
    return jax.nn.gelu(x, approximate=True)

def _silu(x):
    return jax.nn.silu(x)

def _sigmoid(x):
    return jax.nn.sigmoid(x)

def _layernorm(x, axis=-1, eps=1e-05):
    m = jnp.mean(x, axis=axis, keepdims=True)
    v = jnp.var(x, axis=axis, keepdims=True)
    return (x - m) / jnp.sqrt(v + eps)

def _scatter_add(tgt, idx, src, axis=0):
    return tgt.at[idx].add(src)

def _segment_sum(src, seg, n):
    return jax.ops.segment_sum(src, seg, n)
kernel_name = 'mk_prb_d1_jaxref_r2_d75040'

def setup_inputs(seed: int=0):
    np.random.seed(seed)
    _w = jnp.asarray

    def _L0_attn_setup():
        import jax, jax.numpy as jnp
        import numpy as np
        NHEAD = 16

        def _forward(x, time_maa_x, time_maa, time_maa_w1, time_maa_w2, time_decay, time_decay_w1, time_decay_w2, time_aaaaa, time_aaa_w1, time_aaa_w2, time_kkk_w1, time_kkk_w2, gate_w1, gate_w2, time_misc_a, ma_w1, ma_w2, time_misc_k, mk_w1, mk_w2, receptance, key_w, value, output, ln_w, ln_b, time_faaaa):
            B, T, C = x.shape
            H, N = (NHEAD, C // NHEAD)
            xprev = jnp.pad(x, ((0, 0), (1, 0), (0, 0)))[:, :T]
            xx = xprev - x
            xxx = x + xx * time_maa_x
            mix = jnp.tanh(xxx @ time_maa_w1.T).reshape(B, T, 4, -1)
            deltas = jnp.einsum('btfd,fcd->fbtc', mix, time_maa_w2)
            xrg, xwa, xk, xv = x[None] + xx[None] * (time_maa + deltas)
            r = xrg @ receptance.T
            g = jnp.tanh(xrg @ gate_w1.T) @ gate_w2.T
            k = xk @ key_w.T
            kk1 = jnp.tanh(xk @ time_kkk_w1.T)
            mk1 = xk @ mk_w1.T
            v = xv @ value.T
            w1 = jnp.tanh(xwa @ time_decay_w1.T)
            a1 = xwa @ time_aaa_w1.T
            ma1 = xwa @ ma_w1.T
            w = -jax.nn.softplus(-(time_decay + w1 @ time_decay_w2.T)) - 0.5
            kk = k + kk1 @ time_kkk_w2.T
            kk = kk.reshape(B, T, H, N)
            kk = kk / jnp.maximum(jnp.linalg.norm(kk, axis=-1, keepdims=True), 1e-12)
            kk = kk.reshape(B, T, C)
            a = jax.nn.sigmoid(time_aaaaa + a1 @ time_aaa_w2.T)
            ma = jax.nn.sigmoid(time_misc_a + ma1 @ ma_w2.T)
            k = k * ma + k * a * (1 - ma)
            mk = jax.nn.sigmoid(time_misc_k + mk1 @ mk_w2.T)
            k = k * jnp.exp(w * mk)
            b = -kk * a

            def heads(z):
                return z.reshape(B, T, H, N).transpose(1, 0, 2, 3)
            rh, wh, kh, vh, kkh, bh = map(heads, (r, w, k, v, kk, b))

            def step(S, inp):
                r_, w_, k_, v_, kk_, b_ = inp
                sab = jnp.einsum('bhvk,bhk->bhv', S, kk_)
                S = S * jnp.exp(w_)[:, :, None, :] + sab[..., None] * b_[:, :, None, :] + v_[..., None] * k_[:, :, None, :]
                y = jnp.einsum('bhvk,bhk->bhv', S, r_)
                return (S, y)
            S0 = jnp.zeros((B, H, N, N), x.dtype)
            _, y = jax.lax.scan(step, S0, (rh, wh, kh, vh, kkh, bh))
            y = y.transpose(1, 0, 2, 3)
            mu = y.mean(-1, keepdims=True)
            var = ((y - mu) ** 2).mean(-1, keepdims=True)
            yn = (y - mu) / jnp.sqrt(var + 0.00064) * ln_w.reshape(H, N) + ln_b.reshape(H, N)
            r4 = r.reshape(B, T, H, N)
            k4 = k.reshape(B, T, H, N)
            v4 = v.reshape(B, T, H, N)
            bonus = (r4 * k4 * time_faaaa.reshape(H, N)).sum(-1, keepdims=True) * v4
            out = (yn + bonus).reshape(B, T, C) * g
            return out @ output.T
        key = jax.random.key(seed)
        ks = iter(jax.random.split(key, 40))
        B, T, C = (2, 512, 512)

        def n(shape, s=1.0):
            return jax.random.normal(next(ks), shape, jnp.float32) * s

        def u(shape, lo, hi):
            return jax.random.uniform(next(ks), shape, jnp.float32, lo, hi)
        d = {}
        d['x'] = n((B, T, C))
        d['time_maa_x'] = u((1, 1, C), 0.0, 1.0)
        d['time_maa'] = u((4, 1, 1, C), 0.0, 1.0)
        d['time_maa_w1'] = n((128, C), 0.02)
        d['time_maa_w2'] = n((4, C, 32), 0.05)
        d['time_decay'] = u((1, 1, C), -6.5, -1.5)
        d['time_decay_w1'] = n((64, C), 0.02)
        d['time_decay_w2'] = n((C, 64), 0.05)
        d['time_aaaaa'] = n((1, 1, C), 0.1)
        d['time_aaa_w1'] = n((16, C), 0.02)
        d['time_aaa_w2'] = n((C, 16), 0.05)
        d['time_kkk_w1'] = n((16, C), 0.02)
        d['time_kkk_w2'] = n((C, 16), 0.05)
        d['gate_w1'] = n((128, C), 0.05)
        d['gate_w2'] = n((C, 128), 0.05)
        d['time_misc_a'] = n((1, 1, C), 0.1)
        d['ma_w1'] = n((16, C), 0.02)
        d['ma_w2'] = n((C, 16), 0.05)
        d['time_misc_k'] = n((1, 1, C), 0.1)
        d['mk_w1'] = n((16, C), 0.02)
        d['mk_w2'] = n((C, 16), 0.05)
        s = 0.5 / C ** 0.5
        d['receptance'] = u((C, C), -s, s)
        d['key_w'] = u((C, C), -0.1 * s, 0.1 * s)
        d['value'] = u((C, C), -s, s)
        d['output'] = n((C, C), 0.02)
        d['ln_w'] = jnp.ones((C,), jnp.float32)
        d['ln_b'] = jnp.zeros((C,), jnp.float32)
        d['time_faaaa'] = n((C,), 0.1)
        return d
    _L0_attn_in = _L0_attn_setup()

    def _L0_ffn_setup():
        import jax, jax.numpy as jnp
        import numpy as np
        LN_EPS = 1e-05

        def layer_norm(x, g, b):
            mu = jnp.mean(x, axis=-1, keepdims=True)
            var = jnp.var(x, axis=-1, keepdims=True)
            return (x - mu) / jnp.sqrt(var + LN_EPS) * g + b

        def balanced_assignment(scores):
            T, E = scores.shape
            C = T // E
            taken = jnp.zeros((T,), dtype=bool)
            parts = []
            for e in range(E):
                s = jnp.where(taken, -jnp.inf, scores[:, e])
                _, idx = jax.lax.top_k(s, C)
                parts.append(idx)
                taken = taken.at[idx].set(True)
            return jnp.concatenate(parts)
        key = jax.random.key(seed)
        ks = jax.random.split(key, 4)
        B, S, D, F, E = (4, 1024, 512, 2048, 8)
        return {'x': jax.random.normal(ks[0], (B, S, D), dtype=jnp.float32), 'centroids': jax.random.normal(ks[1], (E, D), dtype=jnp.float32) * 0.1, 'ln_g': jnp.ones((D,), dtype=jnp.float32), 'ln_b': jnp.zeros((D,), dtype=jnp.float32), 'w1': jax.random.normal(ks[2], (E, D, F), dtype=jnp.float32) * 0.02, 'b1': jnp.zeros((E, F), dtype=jnp.float32), 'w2': jax.random.normal(ks[3], (E, F, D), dtype=jnp.float32) * 0.02, 'b2': jnp.zeros((E, D), dtype=jnp.float32)}
    _L0_ffn_in = _L0_ffn_setup()
    _d = {'L0_attn_x': _L0_attn_in['x'], 'L0_attn_time_maa_x': _L0_attn_in['time_maa_x'], 'L0_attn_time_maa': _L0_attn_in['time_maa'], 'L0_attn_time_maa_w1': _L0_attn_in['time_maa_w1'], 'L0_attn_time_maa_w2': _L0_attn_in['time_maa_w2'], 'L0_attn_time_decay': _L0_attn_in['time_decay'], 'L0_attn_time_decay_w1': _L0_attn_in['time_decay_w1'], 'L0_attn_time_decay_w2': _L0_attn_in['time_decay_w2'], 'L0_attn_time_aaaaa': _L0_attn_in['time_aaaaa'], 'L0_attn_time_aaa_w1': _L0_attn_in['time_aaa_w1'], 'L0_attn_time_aaa_w2': _L0_attn_in['time_aaa_w2'], 'L0_attn_time_kkk_w1': _L0_attn_in['time_kkk_w1'], 'L0_attn_time_kkk_w2': _L0_attn_in['time_kkk_w2'], 'L0_attn_gate_w1': _L0_attn_in['gate_w1'], 'L0_attn_gate_w2': _L0_attn_in['gate_w2'], 'L0_attn_time_misc_a': _L0_attn_in['time_misc_a'], 'L0_attn_ma_w1': _L0_attn_in['ma_w1'], 'L0_attn_ma_w2': _L0_attn_in['ma_w2'], 'L0_attn_time_misc_k': _L0_attn_in['time_misc_k'], 'L0_attn_mk_w1': _L0_attn_in['mk_w1'], 'L0_attn_mk_w2': _L0_attn_in['mk_w2'], 'L0_attn_receptance': _L0_attn_in['receptance'], 'L0_attn_key_w': _L0_attn_in['key_w'], 'L0_attn_value': _L0_attn_in['value'], 'L0_attn_output': _L0_attn_in['output'], 'L0_attn_ln_w': _L0_attn_in['ln_w'], 'L0_attn_ln_b': _L0_attn_in['ln_b'], 'L0_attn_time_faaaa': _L0_attn_in['time_faaaa'], 'L0_ffn_centroids': _L0_ffn_in['centroids'], 'L0_ffn_ln_g': _L0_ffn_in['ln_g'], 'L0_ffn_ln_b': _L0_ffn_in['ln_b'], 'L0_ffn_w1': _L0_ffn_in['w1'], 'L0_ffn_b1': _L0_ffn_in['b1'], 'L0_ffn_w2': _L0_ffn_in['w2'], 'L0_ffn_b2': _L0_ffn_in['b2']}
    _x0 = _d['L0_attn_x']
    _d['L0_attn_x'] = jax.random.normal(jax.random.fold_in(jax.random.key(seed), 1), (2, 4096, 512), dtype=_x0.dtype)
    del _x0
    return _d

def reference(L0_attn_x, L0_attn_time_maa_x, L0_attn_time_maa, L0_attn_time_maa_w1, L0_attn_time_maa_w2, L0_attn_time_decay, L0_attn_time_decay_w1, L0_attn_time_decay_w2, L0_attn_time_aaaaa, L0_attn_time_aaa_w1, L0_attn_time_aaa_w2, L0_attn_time_kkk_w1, L0_attn_time_kkk_w2, L0_attn_gate_w1, L0_attn_gate_w2, L0_attn_time_misc_a, L0_attn_ma_w1, L0_attn_ma_w2, L0_attn_time_misc_k, L0_attn_mk_w1, L0_attn_mk_w2, L0_attn_receptance, L0_attn_key_w, L0_attn_value, L0_attn_output, L0_attn_ln_w, L0_attn_ln_b, L0_attn_time_faaaa, L0_ffn_centroids, L0_ffn_ln_g, L0_ffn_ln_b, L0_ffn_w1, L0_ffn_b1, L0_ffn_w2, L0_ffn_b2):

    def _L0_attn_ref(x, time_maa_x, time_maa, time_maa_w1, time_maa_w2, time_decay, time_decay_w1, time_decay_w2, time_aaaaa, time_aaa_w1, time_aaa_w2, time_kkk_w1, time_kkk_w2, gate_w1, gate_w2, time_misc_a, ma_w1, ma_w2, time_misc_k, mk_w1, mk_w2, receptance, key_w, value, output, ln_w, ln_b, time_faaaa):
        import jax, jax.numpy as jnp
        import numpy as np
        NHEAD = 16

        def _forward(x, time_maa_x, time_maa, time_maa_w1, time_maa_w2, time_decay, time_decay_w1, time_decay_w2, time_aaaaa, time_aaa_w1, time_aaa_w2, time_kkk_w1, time_kkk_w2, gate_w1, gate_w2, time_misc_a, ma_w1, ma_w2, time_misc_k, mk_w1, mk_w2, receptance, key_w, value, output, ln_w, ln_b, time_faaaa):
            B, T, C = x.shape
            H, N = (NHEAD, C // NHEAD)
            xprev = jnp.pad(x, ((0, 0), (1, 0), (0, 0)))[:, :T]
            xx = xprev - x
            xxx = x + xx * time_maa_x
            mix = jnp.tanh(xxx @ time_maa_w1.T).reshape(B, T, 4, -1)
            deltas = jnp.einsum('btfd,fcd->fbtc', mix, time_maa_w2)
            xrg, xwa, xk, xv = x[None] + xx[None] * (time_maa + deltas)
            r = xrg @ receptance.T
            g = jnp.tanh(xrg @ gate_w1.T) @ gate_w2.T
            k = xk @ key_w.T
            kk1 = jnp.tanh(xk @ time_kkk_w1.T)
            mk1 = xk @ mk_w1.T
            v = xv @ value.T
            w1 = jnp.tanh(xwa @ time_decay_w1.T)
            a1 = xwa @ time_aaa_w1.T
            ma1 = xwa @ ma_w1.T
            w = -jax.nn.softplus(-(time_decay + w1 @ time_decay_w2.T)) - 0.5
            kk = k + kk1 @ time_kkk_w2.T
            kk = kk.reshape(B, T, H, N)
            kk = kk / jnp.maximum(jnp.linalg.norm(kk, axis=-1, keepdims=True), 1e-12)
            kk = kk.reshape(B, T, C)
            a = jax.nn.sigmoid(time_aaaaa + a1 @ time_aaa_w2.T)
            ma = jax.nn.sigmoid(time_misc_a + ma1 @ ma_w2.T)
            k = k * ma + k * a * (1 - ma)
            mk = jax.nn.sigmoid(time_misc_k + mk1 @ mk_w2.T)
            k = k * jnp.exp(w * mk)
            b = -kk * a

            def heads(z):
                return z.reshape(B, T, H, N).transpose(1, 0, 2, 3)
            rh, wh, kh, vh, kkh, bh = map(heads, (r, w, k, v, kk, b))

            def step(S, inp):
                r_, w_, k_, v_, kk_, b_ = inp
                sab = jnp.einsum('bhvk,bhk->bhv', S, kk_)
                S = S * jnp.exp(w_)[:, :, None, :] + sab[..., None] * b_[:, :, None, :] + v_[..., None] * k_[:, :, None, :]
                y = jnp.einsum('bhvk,bhk->bhv', S, r_)
                return (S, y)
            S0 = jnp.zeros((B, H, N, N), x.dtype)
            _, y = jax.lax.scan(step, S0, (rh, wh, kh, vh, kkh, bh))
            y = y.transpose(1, 0, 2, 3)
            mu = y.mean(-1, keepdims=True)
            var = ((y - mu) ** 2).mean(-1, keepdims=True)
            yn = (y - mu) / jnp.sqrt(var + 0.00064) * ln_w.reshape(H, N) + ln_b.reshape(H, N)
            r4 = r.reshape(B, T, H, N)
            k4 = k.reshape(B, T, H, N)
            v4 = v.reshape(B, T, H, N)
            bonus = (r4 * k4 * time_faaaa.reshape(H, N)).sum(-1, keepdims=True) * v4
            out = (yn + bonus).reshape(B, T, C) * g
            return out @ output.T
        return _forward(x, time_maa_x, time_maa, time_maa_w1, time_maa_w2, time_decay, time_decay_w1, time_decay_w2, time_aaaaa, time_aaa_w1, time_aaa_w2, time_kkk_w1, time_kkk_w2, gate_w1, gate_w2, time_misc_a, ma_w1, ma_w2, time_misc_k, mk_w1, mk_w2, receptance, key_w, value, output, ln_w, ln_b, time_faaaa)

    def _L0_ffn_ref(x, centroids, ln_g, ln_b, w1, b1, w2, b2):
        import jax, jax.numpy as jnp
        import numpy as np
        LN_EPS = 1e-05

        def layer_norm(x, g, b):
            mu = jnp.mean(x, axis=-1, keepdims=True)
            var = jnp.var(x, axis=-1, keepdims=True)
            return (x - mu) / jnp.sqrt(var + LN_EPS) * g + b

        def balanced_assignment(scores):
            T, E = scores.shape
            C = T // E
            taken = jnp.zeros((T,), dtype=bool)
            parts = []
            for e in range(E):
                s = jnp.where(taken, -jnp.inf, scores[:, e])
                _, idx = jax.lax.top_k(s, C)
                parts.append(idx)
                taken = taken.at[idx].set(True)
            return jnp.concatenate(parts)
        D = x.shape[-1]
        feat = x.reshape(-1, D)
        T = feat.shape[0]
        E = centroids.shape[0]
        C = T // E
        norm = layer_norm(feat, ln_g, ln_b)
        scores = jax.lax.stop_gradient(norm @ centroids.T)
        sort_by_expert = balanced_assignment(scores)
        routed = feat[sort_by_expert].reshape(E, C, D)
        h = layer_norm(routed, ln_g, ln_b)
        h = jax.nn.gelu(jnp.einsum('ecd,edf->ecf', h, w1) + b1[:, None, :])
        h = jnp.einsum('ecf,efd->ecd', h, w2) + b2[:, None, :]
        out = routed + h
        inv = jnp.zeros((T,), dtype=jnp.int32).at[sort_by_expert].set(jnp.arange(T, dtype=jnp.int32))
        return out.reshape(T, D)[inv].reshape(x.shape)
    x = L0_attn_x
    xn = _layernorm(x, axis=-1)
    x = x + _L0_attn_ref(xn, L0_attn_time_maa_x, L0_attn_time_maa, L0_attn_time_maa_w1, L0_attn_time_maa_w2, L0_attn_time_decay, L0_attn_time_decay_w1, L0_attn_time_decay_w2, L0_attn_time_aaaaa, L0_attn_time_aaa_w1, L0_attn_time_aaa_w2, L0_attn_time_kkk_w1, L0_attn_time_kkk_w2, L0_attn_gate_w1, L0_attn_gate_w2, L0_attn_time_misc_a, L0_attn_ma_w1, L0_attn_ma_w2, L0_attn_time_misc_k, L0_attn_mk_w1, L0_attn_mk_w2, L0_attn_receptance, L0_attn_key_w, L0_attn_value, L0_attn_output, L0_attn_ln_w, L0_attn_ln_b, L0_attn_time_faaaa) + _L0_ffn_ref(xn, L0_ffn_centroids, L0_ffn_ln_g, L0_ffn_ln_b, L0_ffn_w1, L0_ffn_b1, L0_ffn_w2, L0_ffn_b2)
    return x

_drawn_inputs = setup_inputs


def setup_inputs(seed=0):
    import zlib

    import numpy as np

    out = dict(_drawn_inputs(seed))
    spreads = {'L0_attn_ln_w': (1.0, 0.2),
     'L0_attn_ln_b': (0.0, 0.1),
     'L0_ffn_ln_g': (1.0, 0.2),
     'L0_ffn_ln_b': (0.0, 0.1),
     'L0_ffn_b1': (0.0, 0.1),
     'L0_ffn_b2': (0.0, 0.1)}
    factors = {}
    for name, (base, spread) in spreads.items():
        noise = np.random.default_rng([zlib.crc32(name.encode()), seed]).standard_normal(out[name].shape)
        drawn = base * np.exp(spread * noise) if base else spread * noise
        out[name] = jnp.asarray(drawn.astype(out[name].dtype))
    for name, factor in factors.items():
        out[name] = (out[name] * factor).astype(out[name].dtype)
    return out
```

```python
import numpy as np
import concourse.bass as bass
from concourse import mybir
from contextlib import ExitStack

F32, I32 = mybir.dt.float32, mybir.dt.int32
ALU, ACT, AX = mybir.AluOpType, mybir.ActivationFunctionType, mybir.AxisListType

P = 128
B, T, C = 2, 4096, 512
NT = B * T
G = C // P
N = 32
HG = P // N
E, F = 8, 2048
CAP = NT // E
EPS = 1e-5


class Queue:

    def __init__(self, engine, sem):
        self.e, self.sem, self.n, self.seen = engine, sem, 0, {}

    def did(self, instruction):
        instruction.then_inc(self.sem, 1)
        self.n += 1
        return self.sem, self.n

    def wait(self, *steps):
        for step in steps:
            if step is not None and self.seen.get(step[0].name, 0) < step[1]:
                self.seen[step[0].name] = step[1]
                self.e.wait_ge(*step)


class Core:

    def __init__(self, nc, ctx):
        self.nc, self.ctx, self.streams, self.counts = nc, ctx, {}, {}
        queue = lambda e, name: Queue(e, ctx.enter_context(nc.semaphore(name)))
        self.pe, self.dve = queue(nc.tensor, "pe_steps"), queue(nc.vector, "dve_steps")
        self.act, self.pool = queue(nc.scalar, "act_steps"), queue(nc.gpsimd, "pool_steps")
        self.sp = queue(nc.sync, "sp_steps")
        self.scattered, self.got_h, self.got_acc, self.stored = (
            ctx.enter_context(nc.semaphore(n)) for n in ("scattered", "got_h", "got_acc", "stored"))
        self.tick = ctx.enter_context(nc.sbuf_tensor("tick", [P, 1], F32))
        nc.gpsimd.memset(self.tick[:, :], 0.0).then_inc(self.pool.sem, 1)
        self.pool.n = 1
        self.queues = (self.pe, self.dve, self.act, self.pool, self.sp)

    def dma(self, queue, stream, out, in_):
        return self.landed(stream, queue.e.dma_start(out, in_))

    def landed(self, stream, instruction):
        if stream not in self.streams:
            self.streams[stream] = self.ctx.enter_context(self.nc.semaphore("dma_" + stream))
            self.counts[stream] = 0
        self.counts[stream] += 16
        instruction.then_inc(self.streams[stream], 16)
        return self.streams[stream], self.counts[stream]

    def pool_sees(self, counter, value):
        pool = self.pool
        pool.e.wait_ge(pool.sem, pool.n)
        pool.e.wait_ge(counter, value)
        return pool.did(pool.e.tensor_tensor(self.tick[:, :], self.tick[:, :], self.tick[:, :], ALU.add))

    def meet(self):
        for name, count in self.counts.items():
            if count:
                self.sp.wait((self.streams[name], count))
        for q in self.queues:
            if q.n:
                q.e.wait_ge(q.sem, q.n)
        self.nc.all_engine_barrier()
        for q in self.queues:
            if q.n:
                self.nc.sync.sem_clear(q.sem)
        for name, count in self.counts.items():
            if count:
                self.nc.sync.sem_clear(self.streams[name])
        self.nc.all_engine_barrier()
        for q in self.queues:
            q.n, q.seen = 0, {}
        self.counts = dict.fromkeys(self.counts, 0)


def norm_and_scores(nc, core, dram):
    pe, dve, act, pool, sp = core.queues
    SUB = 4
    with ExitStack() as ctx:
        sb = lambda name, shape, dt=F32: ctx.enter_context(nc.sbuf_tensor(name, shape, dt))
        x, xn, h0, h, hT = (sb(f"a_{n}", [P, SUB, C]) for n in ("x", "xn", "h0", "h", "hT"))
        gain, bias, cent = sb("a_gain", [P, C]), sb("a_bias", [P, C]), sb("a_cent", [P, G, E])
        ident = sb("a_ident", [P, P])
        stats, mv, var, std, rstd = (sb(f"a_{n}", [P, 2, SUB, k]) for n, k in (
            ("stats", 6), ("mv", 2), ("var", 1), ("std", 1), ("rstd", 1)))
        scores = sb("a_scores", [P, SUB, E])
        turn = [ctx.enter_context(nc.psum_tensor(f"a_turn{i}", [P, C], F32)) for i in range(2)]
        score_ps = ctx.enter_context(nc.psum_tensor("a_score_ps", [P, SUB, E], F32))
        core.dma(sp, "const", gain[:, :], dram["ln_g"].to_broadcast([P, C]))
        core.dma(sp, "const", bias[:, :], dram["ln_b"].to_broadcast([P, C]))
        core.dma(sp, "const", cent[:, :, :], dram["centT"])
        core.dma(sp, "const", ident[:, :], dram["ident"])
        core.meet()
        rows = lambda a, i: a.rearrange("(i s p) c -> i p s c", s=SUB, p=P)[bass.ds(i, 1)].rearrange(
            "o p s c -> (o p) s c")
        with nc.Fori(0, NT // (SUB * P)) as i:
            x_in = core.dma(sp, "x", x[:, :, :], rows(dram["x"], i))

            def normalise(which, src, dst, ready):
                dve.wait(ready)
                for s in range(SUB):
                    got = dve.did(dve.e.bn_stats(stats[:, which, s], src[:, s]))
                dve.wait(got)
                for s in range(SUB):
                    got = dve.did(dve.e.bn_aggr(mv[:, which, s], stats[:, which, s]))
                dve.wait(got)
                got = dve.did(dve.e.tensor_scalar(var[:, which, :, 0], mv[:, which, :, 1], EPS, None, ALU.add))
                act.wait(got)
                got = act.did(act.e.activation(std[:, which, :, 0], var[:, which, :, 0], ACT.Sqrt))
                dve.wait(got)
                got = dve.did(dve.e.reciprocal(rstd[:, which, :, 0], std[:, which, :, 0]))
                dve.wait(got)
                for s in range(SUB):
                    got = dve.did(dve.e.tensor_scalar(dst[:, s], src[:, s], mv[:, which, s, 0:1],
                                                      rstd[:, which, s], ALU.subtract, ALU.mult))
                return got

            xn_done = normalise(0, x, xn, x_in)
            sp.wait(xn_done)
            core.dma(sp, "xn", rows(dram["xn"], i), xn[:, :, :])
            h0_done = normalise(1, xn, h0, xn_done)
            dve.wait(h0_done)
            bc = lambda a: a[:, :].rearrange("p (s c) -> p s c", s=1).to_broadcast([P, SUB, C])
            gained = dve.did(dve.e.tensor_tensor(h0[:, :, :], h0[:, :, :], bc(gain), ALU.mult))
            dve.wait(gained)
            h_done = dve.did(dve.e.tensor_tensor(h[:, :, :], h0[:, :, :], bc(bias), ALU.add))
            sp.wait(h_done)
            core.dma(sp, "h", rows(dram["h"], i), h[:, :, :])
            pe.wait(h_done)
            copied = {}
            for s in range(SUB):
                pe.wait(copied.get(s - 2))
                for g in range(G):
                    turned = pe.did(pe.e.transpose(turn[s % 2][:, g * P:(g + 1) * P],
                                                   h[:, s, g * P:(g + 1) * P], ident[:, :]))
                act.wait(turned)
                copied[s] = act.did(act.e.copy(hT[:, s], turn[s % 2][:, :]))
            for s in range(SUB):
                pe.wait(copied[s])
                for g in range(G):
                    mm = pe.e.matmul(score_ps[:, s], hT[:, s, g * P:(g + 1) * P], cent[:, g],
                                     start=g == 0, stop=g == G - 1)
            scored = pe.did(mm)
            dve.wait(scored)
            out = dve.did(dve.e.tensor_copy(scores[:, :, :], score_ps[:, :, :]))
            sp.wait(out)
            core.dma(sp, "scores", dram["scores"].rearrange("(i s p) e -> i p s e", s=SUB, p=P)[
                bass.ds(i, 1)].rearrange("o p s e -> (o p) s e"), scores[:, :, :])
            core.meet()


def route(nc, core, dram):
    pe, dve, act, pool, sp = core.queues
    TT = NT // P
    J = 15
    with ExitStack() as ctx:
        sb = lambda name, shape, dt=F32: ctx.enter_context(nc.sbuf_tensor(name, shape, dt))
        score = sb("r_score", [P, TT, E])
        sign, key, part = (sb(f"r_{n}", [P, TT, E], I32) for n in ("sign", "key", "part"))
        hi, lo = sb("r_hi", [P, E, TT]), sb("r_lo", [P, E, TT])
        free, slot, hi_e, lo_e = (sb(f"r_{n}", [P, TT]) for n in ("free", "slot", "hi_e", "lo_e"))
        above, equal, tie, rank, scan, tmp = (sb(f"r_{n}", [P, TT]) for n in (
            "above", "equal", "tie", "rank", "scan", "tmp"))
        ge, cand, cnt, steps15 = sb("r_ge", [P, J, TT]), sb("r_cand", [P, J]), sb("r_cnt", [P, J]), sb("r_15", [P, J])
        cur_hi, cur_lo, nsel, need, base, ones1 = (sb(f"r_{n}", [P, 1]) for n in (
            "cur_hi", "cur_lo", "nsel", "need", "base", "ones1"))
        junk = sb("r_junk", [P, J])
        onesT = sb("r_onesT", [P, TT])
        ones, before = sb("r_ones", [P, P]), sb("r_before", [P, P])
        slot_i, ids, slot8, ids8 = (sb(f"r_{n}", s, I32) for n, s in (
            ("slot_i", [P, TT]), ("ids", [P, TT]), ("slot8", [P, 8]), ("ids8", [P, 8])))
        ps = ctx.enter_context(nc.psum_tensor("r_ps", [P, 2, TT], F32))
        cps = ctx.enter_context(nc.psum_tensor("r_cps", [P, J], F32))

        def step(q, instruction):
            done = q.did(instruction)
            q.wait(done)
            return done

        core.dma(sp, "const", score[:, :, :], dram["scores"].rearrange("(t p) e -> p t e", p=P))
        core.dma(sp, "const", ones[:, :], dram["ones"])
        core.dma(sp, "const", before[:, :], dram["before"])
        core.dma(sp, "const", steps15[:, :], dram["steps15"])
        step(pool, pool.e.iota(ids[:, :], pattern=[[P, TT]], base=0, channel_multiplier=1))
        for a, v in ((free, 1.0), (slot, 0.0), (base, 0.0), (ones1, 1.0), (onesT, 1.0)):
            step(dve, dve.e.memset(a[:, :], v))
        core.meet()
        bits = score[:, :, :].bitcast(I32)
        step(dve, dve.e.tensor_scalar(sign[:, :, :], bits, 31, -2147483648, ALU.arith_shift_right, ALU.bitwise_or))
        step(dve, dve.e.tensor_tensor(key[:, :, :], bits, sign[:, :, :], ALU.bitwise_xor))
        step(dve, dve.e.tensor_scalar(part[:, :, :], key[:, :, :], 16, None, ALU.logical_shift_right))
        step(dve, dve.e.tensor_copy(hi[:, :, :].rearrange("p e t -> p t e"), part[:, :, :]))
        step(dve, dve.e.tensor_scalar(part[:, :, :], key[:, :, :], 65535, None, ALU.bitwise_and))
        step(dve, dve.e.tensor_copy(lo[:, :, :].rearrange("p e t -> p t e"), part[:, :, :]))
        core.meet()

        def total(mask, out):
            step(dve, dve.e.tensor_reduce(cnt[:, 0:1], mask[:, :], AX.X, ALU.add))
            pe.wait((dve.sem, dve.n))
            got = pe.did(pe.e.matmul(cps[:, 0:1], ones[:, :], cnt[:, 0:1], start=True, stop=True))
            dve.wait(got)
            step(dve, dve.e.tensor_copy(out[:, :], cps[:, 0:1]))

        def search(values, wanted, cur):
            step(dve, dve.e.memset(cur[:, :], 0.0))
            for bit in (12, 8, 4, 0):
                size = float(1 << bit)
                step(dve, dve.e.tensor_scalar(cand[:, :], steps15[:, :], size, cur[:, 0:1], ALU.mult, ALU.add))
                step(dve, dve.e.tensor_tensor(
                    ge[:, :, :], values[:, :].rearrange("p (j t) -> p j t", j=1).to_broadcast([P, J, TT]),
                    cand[:, :].rearrange("p (j t) -> p j t", t=1).to_broadcast([P, J, TT]), ALU.is_ge))
                step(dve, dve.e.tensor_reduce(cnt[:, :], ge[:, :, :], AX.X, ALU.add))
                pe.wait((dve.sem, dve.n))
                got = pe.did(pe.e.matmul(cps[:, :], ones[:, :], cnt[:, :], start=True, stop=True))
                dve.wait(got)
                step(dve, dve.e.tensor_scalar(junk[:, :], cps[:, :], wanted, None, ALU.is_ge, ALU.add,
                                              accum_out=nsel[:, :]))
                step(dve, dve.e.scalar_tensor_tensor(cur[:, :], nsel[:, :], size, cur[:, :], ALU.mult, ALU.add))

        def ranks(mask):
            pe.wait((dve.sem, dve.n))
            pe.e.matmul(ps[:, 0], before[:, :], mask[:, :], start=True, stop=True)
            got = pe.did(pe.e.matmul(ps[:, 1], ones[:, :], mask[:, :], start=True, stop=True))
            dve.wait(got)
            step(dve, dve.e.tensor_copy(tmp[:, :], ps[:, 1]))
            step(dve, dve.e.tensor_tensor_scan(scan[:, :], onesT[:, :], tmp[:, :], 0.0, ALU.mult, ALU.add))
            step(dve, dve.e.tensor_tensor(scan[:, :], scan[:, :], tmp[:, :], ALU.subtract))
            step(dve, dve.e.tensor_tensor(rank[:, :], ps[:, 0], scan[:, :], ALU.add))

        def masked(out, values, mask):
            step(dve, dve.e.scalar_tensor_tensor(out[:, :], values, 1.0, mask[:, :], ALU.add, ALU.mult))
            step(dve, dve.e.tensor_scalar(out[:, :], out[:, :], -1.0, None, ALU.add))

        with nc.Fori(0, E) as e:
            masked(hi_e, hi[:, bass.ds(e, 1), :].rearrange("p o t -> p (o t)"), free)
            search(hi_e, float(CAP), cur_hi)
            step(dve, dve.e.tensor_scalar(above[:, :], hi_e[:, :], cur_hi[:, 0:1], None, ALU.is_gt))
            step(dve, dve.e.tensor_scalar(equal[:, :], hi_e[:, :], cur_hi[:, 0:1], None, ALU.is_equal))
            total(above, need)
            step(dve, dve.e.tensor_scalar(need[:, :], need[:, :], -1.0, float(CAP), ALU.mult, ALU.add))
            masked(lo_e, lo[:, bass.ds(e, 1), :].rearrange("p o t -> p (o t)"), equal)
            search(lo_e, need[:, 0:1], cur_lo)
            step(dve, dve.e.tensor_scalar(tmp[:, :], lo_e[:, :], cur_lo[:, 0:1], None, ALU.is_gt))
            step(dve, dve.e.tensor_tensor(above[:, :], above[:, :], tmp[:, :], ALU.add))
            step(dve, dve.e.tensor_scalar(tie[:, :], lo_e[:, :], cur_lo[:, 0:1], None, ALU.is_equal))
            total(above, need)
            step(dve, dve.e.tensor_scalar(need[:, :], need[:, :], -1.0, float(CAP), ALU.mult, ALU.add))
            ranks(tie)
            step(dve, dve.e.scalar_tensor_tensor(tie[:, :], rank[:, :], need[:, 0:1], tie[:, :], ALU.is_lt, ALU.mult))
            step(dve, dve.e.tensor_tensor(above[:, :], above[:, :], tie[:, :], ALU.add))
            ranks(above)
            step(dve, dve.e.scalar_tensor_tensor(tmp[:, :], rank[:, :], base[:, 0:1], above[:, :], ALU.add, ALU.mult))
            step(dve, dve.e.tensor_tensor(slot[:, :], slot[:, :], tmp[:, :], ALU.add))
            step(dve, dve.e.tensor_tensor(free[:, :], free[:, :], above[:, :], ALU.subtract))
            step(dve, dve.e.tensor_scalar(base[:, :], base[:, :], float(CAP), None, ALU.add))
            core.meet()
        step(dve, dve.e.tensor_copy(slot_i[:, :], slot[:, :]))
        core.meet()
        with nc.Fori(0, TT // 8) as i:
            dve.did(dve.e.tensor_copy(slot8[:, :], slot_i[:, bass.ds(i * 8, 8)]))
            got = dve.did(dve.e.tensor_copy(ids8[:, :], ids[:, bass.ds(i * 8, 8)]))
            pool.wait(got)
            for j in range(8):
                pool.e.indirect_dma_start(
                    dram["order"], bass.IndirectOffsetOnAxis(ap=slot8[:, j:j + 1], axis=0),
                    ids8[:, j:j + 1], None).then_inc(core.scattered, 16)
            core.pool_sees(core.scattered, i * 128 + 128)
            core.meet()
TB = P // B
NC = TB // N
U = G * B * NC
SU = G * B
W4, W8 = N + N // 2, 6 * 8
FLOOR = -19.5


def time_mix(nc, core, dram):
    pe, dve, act, pool, sp = core.queues
    with ExitStack() as ctx:
        def sb(name, width=G * P, dt=F32):
            return ctx.enter_context(nc.sbuf_tensor("time_" + name, [P, width], dt))

        wt = {}
        for name in ("receptance", "key_w", "value", "output"):
            wt[name] = sb(name, G * C)
        wt["maa_w2"] = sb("maa_w2", 4 * C)
        for name in ("maa_w1", "gate_w1", "gate_w2", "low_wa", "low_k",
                     "decay_w2", "aaa_w2", "ma_w2", "kkk_w2", "mk_w2"):
            wt[name] = sb(name, C)
        for name, width in (("ident", P), ("head_ones", P), ("eye", N), ("one_wa", 1), ("one_k", 1),
                            ("maa_x", G), ("maa", 4 * G), ("faaaa", G), ("ln_w", G), ("ln_b", G),
                            ("restart", G * P), ("pair_u", N), ("pair_uT", N), ("subT", 4 * N)):
            wt[name] = sb(name, width)
        for name, width in (("own_u", N), ("own_y", N), ("prev", 16), ("cross1", 24),
                            ("cross2", 24), ("cross3", 24)):
            wt[name] = sb(name, width, I32)
        for name, tensor in wt.items():
            core.dma(sp, "const", tensor[:, :], dram["w_" + name])

        xn_rows, x_rows, base, acc = sb("xn_rows"), sb("x_rows"), sb("base"), sb("acc")
        x = sb("x", G * B * (TB + 1))
        xx, xxx, lerp, mix = sb("xx"), sb("xxx"), sb("lerp"), sb("mix", P)
        xf = [sb(f"x{f}") for f in ("rg", "wa", "k", "v")]
        r, k, v, gate = sb("r"), sb("k"), sb("v"), sb("gate")
        hid_g, hid_wa, hid_k = sb("hid_g", P), sb("hid_wa", P), sb("hid_k", P)
        zc, soft, wc, w, a, ma, mk = (sb(n) for n in ("zc", "soft", "wc", "w", "a", "ma", "mk"))
        kk, k2, b, bonus = sb("kk"), sb("k2"), sb("b"), sb("bonus")
        sq, norm = sb("sq"), sb("norm")
        csum, cprev = sb("csum"), sb("cprev")
        q = {n: sb(n) for n in ("y4", "u4", "y8", "u8", "ys", "us")}
        diff, grow = [sb("diff0"), sb("diff1")], [sb("grow0"), sb("grow1")]
        key4, key8 = sb("key4", U * 2 * W4), sb("key8", U * 2 * W8)
        k_end, b_end, decay_end = sb("k_end"), sb("b_end"), sb("decay_end", U)
        a_u, a_y, aT_u, aT_y = (sb(n, U * 2 * N) for n in ("a_u", "a_y", "aT_u", "aT_y"))
        inv, sub, part = sb("inv"), sb("sub"), sb("part")
        invT = [sb("invT0"), sb("invT1")]
        kT, bT, vT = sb("kT"), sb("bT"), sb("vT")
        state, faded = sb("state", SU * N), sb("faded", SU * N)
        rhs, corr = sb("rhs", SU * N), sb("corr", SU * N)
        y, mean, var = sb("y"), sb("mean", U), sb("var", U)

        banks = [ctx.enter_context(nc.psum_tensor(f"w_bank{i}", [P, 512], F32)) for i in range(8)]
        last_read = [None] * 8
        taken = [0]

        def bank():
            i = taken[0] % 8
            taken[0] += 1
            pe.wait(last_read[i])
            return i, banks[i]

        def tt(qu, out, in0, in1, op, *needs):
            qu.wait(*needs)
            return qu.did(qu.e.tensor_tensor(out, in0, in1, op))

        def ts(qu, out, in0, s0, s1, op0, op1, *needs):
            qu.wait(*needs)
            return qu.did(qu.e.tensor_scalar(out, in0, s0, s1, op0, op1) if s1 is not None
                          else qu.e.tensor_scalar(out, in0, s0, None, op0))

        def stt(out, in0, s, in1, op0, op1, *needs):
            dve.wait(*needs)
            return dve.did(dve.e.scalar_tensor_tensor(out, in0, s, in1, op0, op1))

        def fn(out, in_, func, *needs, bias=0.0, scale=1.0):
            act.wait(*needs)
            return act.did(act.e.activation(out, in_, func, bias=bias, scale=scale))

        def copy(out, in_, *needs):
            act.wait(*needs)
            return act.did(act.e.copy(out, in_))

        def turn(out, in_, *needs):
            dve.wait(*needs)
            return dve.did(dve.e.transpose(out, in_))

        def project(weight, width, columns, rhs_of, *needs, steps=G):
            i, ps = bank()
            pe.wait(*needs)
            for o in range(len(columns)):
                for g in range(steps):
                    mm = pe.e.matmul(ps[:, o * P:(o + 1) * P],
                                     weight[:, g * width + columns[o]:g * width + columns[o] + P],
                                     rhs_of(g), start=g == 0, stop=g == steps - 1)
            return i, ps, pe.did(mm)

        full = [g * P for g in range(G)]
        col = lambda t: t[:, :]
        grp = lambda t, g: t[:, g * P:(g + 1) * P]
        chunks = lambda t: t[:, :].rearrange("p (n t) -> p n t", t=N)
        fours = lambda t: t[:, :].rearrange("p (q t) -> p q t", t=4)
        eights = lambda t: t[:, :].rearrange("p (q t) -> p q t", t=8)
        per_group = lambda t: t[:, :].rearrange("p (g o) -> p g o", o=1).to_broadcast([P, G, P])
        groups = lambda t: t[:, :].rearrange("p (g c) -> p g c", c=P)
        head = lambda h: slice(h * N, (h + 1) * N)
        blk = lambda n: slice(n * N, (n + 1) * N)

        for t in (x, a_u, a_y, state, hid_k):
            dve.did(dve.e.memset(t[:, :], 0.0))
        core.meet()
        xs = x[:, :].rearrange("p (g b t) -> p g b t", g=G, b=B)
        xnow = xs[:, :, :, 1:TB + 1]
        by_b = lambda t: t[:, :].rearrange("p (g b t) -> p g b t", g=G, b=B)
        tile_rows = lambda a, i, s: a.rearrange("(b i t) c -> b i t c", b=B, t=TB)[s][bass.ds(i, 1)].rearrange(
            "o t c -> (o t) c")

        with nc.Fori(0, T // TB) as i:
            for s in range(B):
                xn_in = core.dma(sp, "w_xn", xn_rows[s * TB:(s + 1) * TB, :], tile_rows(dram["xn"], i, s))
            for s in range(B):
                x_in = core.dma(sp, "w_x", x_rows[s * TB:(s + 1) * TB, :], tile_rows(dram["x"], i, s))
            based = tt(pool, col(base), col(x_rows), col(xn_rows), ALU.add, xn_in, x_in)

            pe.wait(xn_in)
            bi, ps = bank()
            for g in range(G):
                turned = pe.did(pe.e.transpose(ps[:, g * P:(g + 1) * P], grp(xn_rows, g), wt["ident"][:, :]))
            carried = copy(xs[:, :, :, 0:1], xs[:, :, :, TB:TB + 1])
            x_at = last_read[bi] = copy(xnow, by_b(ps), turned, carried)
            xx_at = tt(dve, by_b(xx), xs[:, :, :, 0:TB], xnow, ALU.subtract, x_at)
            dve.wait(xx_at)
            for g in range(G):
                xxx_at = stt(grp(xxx, g).rearrange("p (b t) -> p b t", b=B),
                             grp(xx, g).rearrange("p (b t) -> p b t", b=B), wt["maa_x"][:, g:g + 1],
                             xs[:, g, :, 1:TB + 1], ALU.mult, ALU.add)
            bi, ps, done = project(wt["maa_w1"], P, [0], lambda g: grp(xxx, g), xxx_at)
            mix_at = last_read[bi] = fn(col(mix), ps[:, 0:P], ACT.Tanh, done)
            xf_at = []
            added = None
            for f in range(4):
                bi, ps, done = project(wt["maa_w2"], 0, [f * C + g * P for g in range(G)],
                                       lambda g: col(mix), mix_at, steps=1)
                dve.wait(done, added)
                for g in range(G):
                    lerped = stt(grp(lerp, g), grp(ps, g), wt["maa"][:, f * G + g:f * G + g + 1],
                                 grp(xx, g), ALU.add, ALU.mult)
                last_read[bi] = lerped
                added = tt(dve, by_b(xf[f]), by_b(lerp), xnow, ALU.add, lerped)
                xf_at.append(added)

            bi, ps, done = project(wt["low_wa"], P, [0], lambda g: grp(xf[1], g), xf_at[1])
            wa0 = fn(hid_wa[0:64, :], ps[0:64, 0:P], ACT.Tanh, done)
            wa_at = last_read[bi] = fn(hid_wa[64:P, :], ps[64:P, 0:P], ACT.Identity, bias=wt["one_wa"][64:P, 0:1])
            bi, ps, done = project(wt["low_k"], P, [0], lambda g: grp(xf[2], g), xf_at[2])
            fn(hid_k[0:32, :], ps[0:32, 0:P], ACT.Tanh, done)
            hk_at = last_read[bi] = fn(hid_k[32:64, :], ps[32:64, 0:P], ACT.Identity, bias=wt["one_k"][32:64, 0:1])
            bi, ps, done = project(wt["gate_w1"], P, [0], lambda g: grp(xf[0], g), xf_at[0])
            hg_at = last_read[bi] = fn(col(hid_g), ps[:, 0:P], ACT.Tanh, done)
            bi, ps, done = project(wt["decay_w2"], 0, full, lambda g: col(hid_wa), wa_at, wa0, steps=1)
            z_bank, z = bi, ps
            zc_at = ts(dve, col(zc), col(z), FLOOR, None, ALU.max, None, done)
            below_at = last_read[bi] = tt(dve, col(w), col(z), col(zc), ALU.subtract, zc_at)
            bi, ps, done = project(wt["key_w"], C, full, lambda g: grp(xf[2], g))
            k_at = last_read[bi] = copy(col(k), col(ps), done)
            bi, ps, done = project(wt["kkk_w2"], 0, full, lambda g: col(hid_k), hk_at, steps=1)
            kkr_at = last_read[bi] = tt(dve, col(kk), col(ps), col(k), ALU.add, done, k_at)
            sq_at = tt(pool, col(sq), col(kk), col(kk), ALU.mult, kkr_at)
            bi, ps, done = project(wt["aaa_w2"], 0, full, lambda g: col(hid_wa), steps=1)
            th_a = last_read[bi] = fn(col(a), col(ps), ACT.Tanh, done, scale=0.5)
            bi, ps, done = project(wt["ma_w2"], 0, full, lambda g: col(hid_wa), steps=1)
            th_ma = last_read[bi] = fn(col(ma), col(ps), ACT.Tanh, done, scale=0.5)
            bi, ps, done = project(wt["mk_w2"], 0, full, lambda g: col(hid_k), steps=1)
            th_mk = last_read[bi] = fn(col(mk), col(ps), ACT.Tanh, done, scale=0.5)
            soft_at = fn(col(soft), col(zc), ACT.Exp, zc_at, scale=-1.0)
            bi, ps, done = project(wt["receptance"], C, full, lambda g: grp(xf[0], g))
            r_at = last_read[bi] = copy(col(r), col(ps), done)
            bi, ps, done = project(wt["value"], C, full, lambda g: grp(xf[3], g), xf_at[3])
            v_at = last_read[bi] = copy(col(v), col(ps), done)
            bi, ps, done = project(wt["gate_w2"], 0, full, lambda g: col(hid_g), hg_at, steps=1)
            gate_at = last_read[bi] = copy(col(gate), col(ps), done)

            soft_at = fn(col(soft), col(soft), ACT.Ln, soft_at, bias=1.0)
            wc_at = ts(dve, col(wc), col(soft), -1.0, -0.5, ALU.mult, ALU.add, soft_at)
            w_at = tt(pool, col(w), col(w), col(wc), ALU.add, wc_at, below_at)
            c_at = None
            dve.wait(wc_at)
            c_at = dve.did(dve.e.tensor_tensor_scan(col(csum), wt["restart"][:, :], col(wc), 0.0, ALU.mult, ALU.add))
            cp_at = tt(dve, col(cprev), col(csum), col(wc), ALU.subtract, c_at)
            bi, ps = bank()
            pe.wait(sq_at)
            done = pe.did(pe.e.matmul(ps[:, :], wt["head_ones"][:, :], col(sq), start=True, stop=True))
            n0 = last_read[bi] = ts(dve, col(norm), col(ps), 1e-24, None, ALU.max, None, done)
            dve.wait(n0)
            n1 = dve.did(dve.e.reciprocal(col(norm), col(norm)))
            n2 = fn(col(norm), col(norm), ACT.Sqrt, n1)
            a_at = ts(dve, col(a), col(a), 0.5, 0.5, ALU.mult, ALU.add, th_a)
            ma_at = ts(dve, col(ma), col(ma), 0.5, 0.5, ALU.mult, ALU.add, th_ma)
            mk_at = ts(pool, col(mk), col(mk), 0.5, 0.5, ALU.mult, ALU.add, th_mk)
            wmk_at = tt(pool, col(w), col(w), col(mk), ALU.mult, mk_at, w_at)
            ewmk = fn(col(w), col(w), ACT.Exp, wmk_at)
            kk_at = tt(dve, col(kk), col(kk), col(norm), ALU.mult, n2)
            t0 = stt(col(lerp), col(ma), 1.0, col(a), ALU.subtract, ALU.mult, a_at, ma_at, added)
            t1 = tt(dve, col(lerp), col(ma), col(lerp), ALU.subtract, t0)
            t2 = tt(dve, col(lerp), col(lerp), col(k), ALU.mult, t1)
            k2_at = tt(dve, col(k2), col(lerp), col(w), ALU.mult, t2, ewmk)
            b_at = stt(col(b), col(kk), -1.0, col(a), ALU.mult, ALU.mult, kk_at)
            rk = tt(pool, col(bonus), col(r), col(k2), ALU.mult, r_at, k2_at)
            rk = tt(pool, groups(bonus), groups(bonus), per_group(wt["faaaa"]), ALU.mult, rk)

            mid4 = fours(csum)[:, :, 1:2].to_broadcast([P, G * P // 4, 4])
            first8 = eights(cprev)[:, :, 0:1].to_broadcast([P, G * P // 8, 8])
            turn_at = [None, None]
            use = [0]

            def grown(shape, view, in0, in1, needs, readers, scale=1.0):
                i = use[0] % 2
                use[0] += 1
                d = tt(dve, view(diff[i]), in0, in1, ALU.subtract, turn_at[i], *needs)
                e = fn(shape(grow[i]), shape(diff[i]), ACT.Exp, d, scale=scale)
                turn_at[i] = readers(grow[i], e)
                return i, d

            key4v = key4[:, :].rearrange("p (n s k) -> p n s k", n=U, s=2)
            key8v = key8[:, :].rearrange("p (n s k) -> p n s k", n=U, s=2)
            ready = {}

            def y4_readers(e, at):
                return tt(dve, col(q["y4"]), col(e), col(r), ALU.mult, at)

            i4, d4 = grown(col, fours, fours(csum), mid4, (c_at,), y4_readers)
            e = fn(col(soft), col(diff[i4]), ACT.Exp, d4, wc_at, scale=-1.0)
            tt(dve, key4v[:, :, 1, 0:N], chunks(soft), chunks(k2), ALU.mult, e)
            own = tt(dve, key4v[:, :, 0, 0:N], chunks(soft), chunks(b), ALU.mult)
            turn_at[i4] = own
            grown(col, fours, fours(cprev), mid4, (cp_at,),
                  lambda e, at: tt(dve, col(q["u4"]), col(e), col(kk), ALU.mult, at))
            half = lambda t: t[:, 0:U * 16]
            e16 = lambda t: t[:, 0:U * 16].rearrange("p (n m t) -> p n m t", n=U, m=4)

            def prev_readers(e, at):
                dve.wait(at)
                for s, src in ((1, k2), (0, b)):
                    at = dve.did(dve.e.tensor_tensor(
                        key4v[:, :, s, N:W4].rearrange("p n (m t) -> p n m t", m=4), e16(e),
                        src[:, :].rearrange("p (n m t) -> p n m t", n=U, m=4)[:, :, :, 0:4], ALU.mult))
                return at

            grown(half, lambda t: t[:, 0:U * 16].rearrange("p (q t) -> p q t", t=4),
                  eights(csum)[:, :, 5:6].to_broadcast([P, U * 4, 4]), eights(csum)[:, :, 0:4], (), prev_readers)
            grown(col, eights, eights(csum), first8, (),
                  lambda e, at: tt(dve, col(q["y8"]), col(e), col(r), ALU.mult, at))
            grown(col, eights, eights(cprev), first8, (),
                  lambda e, at: tt(dve, col(q["u8"]), col(e), col(kk), ALU.mult, at))
            offset = 0
            for j in (1, 2, 3):
                n_keys = 8 * j
                view = lambda t: t[:, 0:U * n_keys].rearrange("p (n t) -> p n t", n=U)

                def cross_readers(e, at):
                    dve.wait(at)
                    for s, src in ((1, k2), (0, b)):
                        at = dve.did(dve.e.tensor_tensor(key8v[:, :, s, offset:offset + n_keys], view(e),
                                                         chunks(src)[:, :, 0:n_keys], ALU.mult))
                    return at

                grown(lambda t: t[:, 0:U * n_keys], view,
                      chunks(cprev)[:, :, n_keys:n_keys + 1].to_broadcast([P, U, n_keys]),
                      chunks(csum)[:, :, 0:n_keys], (), cross_readers)
                offset += n_keys
            keys_at = (dve.sem, dve.n)

            e = fn(col(soft), col(csum), ACT.Exp, own, c_at)
            ys_at = tt(dve, col(q["ys"]), col(soft), col(r), ALU.mult, e)
            e = fn(col(zc), col(cprev), ACT.Exp, cp_at, soft_at)
            us_at = tt(dve, col(q["us"]), col(zc), col(kk), ALU.mult, e)
            dend = fn(decay_end[:, :].rearrange("p (n o) -> p n o", o=1), chunks(csum)[:, :, N - 1:N], ACT.Exp)

            def end_readers(e, at):
                tt(dve, col(k_end), col(e), col(k2), ALU.mult, at)
                return tt(dve, col(b_end), col(e), col(b), ALU.mult)

            grown(col, chunks, chunks(csum)[:, :, N - 1:N].to_broadcast([P, U, N]), chunks(csum), (), end_readers)
            end_at = (dve.sem, dve.n)
            kT_at = turn(col(kT), col(k_end), end_at)
            bT_at = turn(col(bT), col(b_end))
            vT_at = turn(col(vT), col(v), v_at)

            def scores(query, keys, width, group):
                bi, ps = bank()
                pe.wait(keys_at)
                for h in range(HG):
                    for m in range(4):
                        n = group * 4 + m
                        mm = pe.e.matmul(ps[head(h), m * 2 * width:(m + 1) * 2 * width], query[head(h), blk(n)],
                                         keys[head(h), n * 2 * width:(n + 1) * 2 * width],
                                         start=m == 0, stop=m == 3, skip_group_check=True)
                return bi, ps, pe.did(mm)

            mask = lambda name, shape, width: wt[name][:, 0:width]
            for group in range(U // 4):
                for dst, who, own_mask in ((a_u, "u", "own_u"), (a_y, "y", "own_y")):
                    d = dst[:, group * 8 * N:(group + 1) * 8 * N].rearrange("p (n t) -> p n t", t=N)
                    bi, ps, done = scores(q[who + "4"], key4, W4, group)
                    src = ps[:, 0:8 * W4].rearrange("p (n k) -> p n k", k=W4)
                    dve.wait(done)
                    m = wt[own_mask][:, :].rearrange("p (o t) -> p o t", o=1).to_broadcast([P, 8, N])
                    own = dve.did(dve.e.copy_predicated(d, m, src[:, :, 0:N]))
                    dve.wait(own)
                    m = wt["prev"][:, :].rearrange("p (o m t) -> p o m t", o=1, m=4).to_broadcast([P, 8, 4, 4])
                    last_read[bi] = dve.did(dve.e.copy_predicated(
                        d.rearrange("p n (m t) -> p n m t", t=8)[:, :, :, 0:4], m,
                        src[:, :, N:W4].rearrange("p n (m t) -> p n m t", m=4)))
                    dve.wait(last_read[bi])
                    bi, ps, done = scores(q[who + "8"], key8, W8, group)
                    src = ps[:, 0:8 * W8].rearrange("p (n k) -> p n k", k=W8)
                    dve.wait(done)
                    offset = 0
                    for j in (1, 2, 3):
                        m = wt[f"cross{j}"][:, 0:8 * j].rearrange("p (o t) -> p o t", o=1).to_broadcast([P, 8, 8 * j])
                        last_read[bi] = dve.did(dve.e.copy_predicated(
                            d[:, :, 0:8 * j], m, src[:, :, offset:offset + 8 * j]))
                        dve.wait(last_read[bi])
                        offset += 8 * j
            aTu_at = turn(col(aT_u), col(a_u))
            aTy_at = turn(col(aT_y), col(a_y))

            a_ub = a_u[:, :].rearrange("p (n s t) -> p n s t", n=U, s=2)[:, :, 0]
            aT_ub = aT_u[:, :].rearrange("p (n s t) -> p n s t", n=U, s=2)[:, :, 0]
            every = lambda m: m.rearrange("p (o t) -> p o t", o=1).to_broadcast([P, U, N])
            t0 = tt(dve, chunks(inv), a_ub, every(wt["pair_u"][:, :]), ALU.mult)
            t1 = tt(dve, chunks(invT[0]), aT_ub, every(wt["pair_uT"][:, :]), ALU.mult, aTu_at)
            t0 = tt(dve, chunks(inv), chunks(inv), every(wt["eye"][:, :]), ALU.add, t0)
            t1 = tt(dve, chunks(invT[0]), chunks(invT[0]), every(wt["eye"][:, :]), ALU.add, t1)

            def blocks_mm(lhsT, rhs_t, *needs):
                bi, ps = bank()
                pe.wait(*needs)
                for n in range(U):
                    for h in range(HG):
                        mm = pe.e.matmul(ps[head(h), blk(n)], lhsT[head(h), blk(n)], rhs_t[head(h), blk(n)],
                                         start=n == 0, stop=n == U - 1, skip_group_check=True)
                return bi, ps, pe.did(mm)

            inv_at, invT_at = t0, t1
            sub_free = None
            for level in range(4):
                old, new = invT[level % 2], invT[(level + 1) % 2]
                s_at = tt(dve, chunks(sub), aT_ub, every(wt["subT"][:, blk(level)]), ALU.mult, sub_free)
                bi, ps, done = blocks_mm(sub, inv, s_at, inv_at)
                sub_free = done
                p_at = last_read[bi] = copy(col(part), col(ps), done)
                bi, ps, done = blocks_mm(part, old, p_at, invT_at)
                invT_at = last_read[bi] = tt(dve, col(new), col(old), col(ps), ALU.add, done)
                if level < 3:
                    inv_at = turn(col(inv), col(new), invT_at)
            solve = invT[0]

            yT = y
            y_at = None
            state_at = None
            copied_y = []
            aTu = lambda n, s: slice((n * 2 + s) * N, (n * 2 + s + 1) * N)
            for c in range(NC):
                nn = [g * NC + c for g in range(SU)]
                bi, ps = bank()
                pe.wait(state_at, aTu_at, aTy_at, us_at, ys_at, vT_at, kT_at, bT_at)
                for u, n in enumerate(nn):
                    for h in range(HG):
                        pe.e.matmul(ps[head(h), blk(u)], aT_u[head(h), aTu(n, 1)], vT[head(h), blk(n)],
                                    start=u == 0, stop=False, skip_group_check=True)
                        mm = pe.e.matmul(ps[head(h), blk(u)], q["us"][head(h), blk(n)], state[head(h), blk(u)],
                                         start=False, stop=u == SU - 1, skip_group_check=True)
                done = pe.did(mm)
                z_at = last_read[bi] = copy(col(rhs), ps[:, 0:SU * N], done)
                faded_at = tt(pool, faded[:, :].rearrange("p (n t) -> p n t", t=N),
                              state[:, :].rearrange("p (n t) -> p n t", t=N),
                              decay_end[:, :].rearrange("p (n c o) -> p n c o", c=NC, o=1)[:, :, c].to_broadcast([P, SU, N]),
                              ALU.mult, dend, state_at)
                bi, ps = bank()
                pe.wait(z_at, invT_at)
                for u, n in enumerate(nn):
                    for h in range(HG):
                        mm = pe.e.matmul(ps[head(h), blk(u)], solve[head(h), blk(n)], rhs[head(h), blk(u)],
                                         start=u == 0, stop=u == SU - 1, skip_group_check=True)
                done = pe.did(mm)
                u_at = last_read[bi] = copy(col(corr), ps[:, 0:SU * N], done)
                ybi, yps = bank()
                sbi, sps = bank()
                pe.wait(u_at)
                for u, n in enumerate(nn):
                    for h in range(HG):
                        hd = head(h)
                        pe.e.matmul(yps[hd, blk(u)], aT_y[hd, aTu(n, 0)], corr[hd, blk(u)],
                                    start=u == 0, stop=False, skip_group_check=True)
                        pe.e.matmul(yps[hd, blk(u)], aT_y[hd, aTu(n, 1)], vT[hd, blk(n)],
                                    start=False, stop=False, skip_group_check=True)
                        pe.e.matmul(yps[hd, blk(u)], q["ys"][hd, blk(n)], state[hd, blk(u)],
                                    start=False, stop=u == SU - 1, skip_group_check=True)
                        pe.e.matmul(sps[hd, blk(u)], bT[hd, blk(n)], corr[hd, blk(u)],
                                    start=u == 0, stop=False, skip_group_check=True)
                        mm = pe.e.matmul(sps[hd, blk(u)], kT[hd, blk(n)], vT[hd, blk(n)],
                                         start=False, stop=u == SU - 1, skip_group_check=True)
                done = pe.did(mm)
                state_at = last_read[sbi] = tt(dve, col(state), col(faded), sps[:, 0:SU * N], ALU.add, done, faded_at)
                y_at = last_read[ybi] = copy(y[:, :].rearrange("p (n c t) -> p n c t", c=NC, t=N)[:, :, c],
                                             yps[:, 0:SU * N].rearrange("p (n t) -> p n t", t=N), done)

            m_of = lambda t: t[:, :].rearrange("p (n o) -> p n o", o=1).to_broadcast([P, U, N])
            dve.wait(y_at)
            s0 = dve.did(dve.e.tensor_reduce(mean[:, :], chunks(y), AX.X, ALU.add))
            s0 = ts(dve, mean[:, :], mean[:, :], 1.0 / N, None, ALU.mult, None, s0)
            c0 = tt(dve, chunks(y), chunks(y), m_of(mean), ALU.subtract, s0)
            s1 = fn(col(sq), col(y), ACT.Square, c0)
            dve.wait(s1)
            s2 = dve.did(dve.e.tensor_reduce(var[:, :], chunks(sq), AX.X, ALU.add))
            s2 = ts(dve, var[:, :], var[:, :], 1.0 / N, 6.4e-4, ALU.mult, ALU.add, s2)
            s3 = fn(var[:, :], var[:, :], ACT.Sqrt, s2)
            dve.wait(s3)
            s4 = dve.did(dve.e.reciprocal(var[:, :], var[:, :]))
            c1 = tt(dve, chunks(y), chunks(y), m_of(var), ALU.mult, s4)
            yc = turn(col(inv), col(y), c1)
            bi, ps = bank()
            pe.wait(rk)
            done = pe.did(pe.e.matmul(ps[:, :], wt["head_ones"][:, :], col(bonus), start=True, stop=True))
            bonus_at = last_read[bi] = tt(dve, col(xxx), col(ps), col(v), ALU.mult, done)
            dve.wait(yc)
            for g in range(G):
                ln_at = dve.did(dve.e.tensor_scalar(grp(part, g), grp(inv, g), wt["ln_w"][:, g:g + 1],
                                                    wt["ln_b"][:, g:g + 1], ALU.mult, ALU.add))
            o0 = tt(dve, col(part), col(part), col(xxx), ALU.add, ln_at, bonus_at)
            o1 = tt(dve, col(part), col(part), col(gate), ALU.mult, o0, gate_at)
            bi, ps = bank()
            pe.wait(o1)
            for g in range(G):
                mm = pe.e.matmul(ps[:, :], grp(part, g), wt["output"][:, g * C:(g + 1) * C], start=g == 0, stop=g == G - 1)
            done = pe.did(mm)
            acc_at = last_read[bi] = tt(dve, col(acc), col(ps), col(base), ALU.add, done, based)
            sp.wait(acc_at)
            for s in range(B):
                core.dma(sp, "w_acc", tile_rows(dram["acc"], i, s), acc[s * TB:(s + 1) * TB, :])
            core.meet()
            for n_ in range(8):
                last_read[n_] = None


def time_mix_inputs(d):
    chan = lambda a: np.ascontiguousarray(a.reshape(G, P).T)
    kin = lambda a: np.ascontiguousarray(
        a.T.reshape(G, P, a.shape[0]).transpose(1, 0, 2).reshape(P, -1))

    def rows(width, *parts):
        out = np.zeros((P, width), np.float32)
        for at, a in parts:
            out[at:at + a.shape[0]] = a
        return out

    low_wa, low_k = np.zeros((P, C), np.float32), np.zeros((P, C), np.float32)
    low_wa[0:64], low_wa[64:80], low_wa[96:112] = d["time_decay_w1"], d["time_aaa_w1"], d["ma_w1"]
    low_k[0:16], low_k[32:48] = d["time_kkk_w1"], d["mk_w1"]
    maa_w2 = np.zeros((4, 32, 4, C), np.float32)
    for f in range(4):
        maa_w2[f, :, f] = d["time_maa_w2"][f].T
    t, i = np.arange(P)[:, None] % N, np.arange(N)[None]
    u16 = np.arange(16)[None]
    same = lambda size: t // size == i // size
    lower = {h: same(2 * h) & (t // h == i // h + 1) for h in (1, 2, 4, 8, 16)}
    upper = {h: same(2 * h) & (t // h == i // h - 1) for h in (1, 2, 4, 8, 16)}
    f32 = lambda a: np.ascontiguousarray(a.astype(np.float32))
    i32 = lambda a: np.ascontiguousarray(a.astype(np.int32))
    hot = lambda at: f32(np.arange(P)[:, None] == at)
    one = lambda name: d[name].reshape(1, C)
    out = {
        "receptance": kin(d["receptance"]), "key_w": kin(d["key_w"]), "value": kin(d["value"]),
        "output": kin(d["output"]), "maa_w1": kin(d["time_maa_w1"]), "gate_w1": kin(d["gate_w1"]),
        "maa_w2": maa_w2.reshape(P, 4 * C), "gate_w2": np.ascontiguousarray(d["gate_w2"].T),
        "low_wa": kin(low_wa), "low_k": kin(low_k),
        "decay_w2": rows(C, (0, d["time_decay_w2"].T), (80, one("time_decay"))),
        "aaa_w2": rows(C, (64, d["time_aaa_w2"].T), (80, one("time_aaaaa"))),
        "ma_w2": rows(C, (96, d["ma_w2"].T), (80, one("time_misc_a"))),
        "kkk_w2": rows(C, (0, d["time_kkk_w2"].T)),
        "mk_w2": rows(C, (32, d["mk_w2"].T), (48, one("time_misc_k"))),
        "ident": np.eye(P, dtype=np.float32),
        "head_ones": f32(np.arange(P)[:, None] // N == np.arange(P)[None] // N),
        "eye": f32(t == i), "one_wa": hot(80), "one_k": hot(48),
        "maa_x": chan(d["time_maa_x"].reshape(C)),
        "maa": np.concatenate([chan(d["time_maa"][f].reshape(C)) for f in range(4)], 1),
        "faaaa": chan(d["time_faaaa"]), "ln_w": chan(d["ln_w"]), "ln_b": chan(d["ln_b"]),
        "restart": f32(np.tile(np.arange(G * P)[None] % N != 0, (P, 1))),
        "pair_u": f32(lower[1]), "pair_uT": f32(upper[1]),
        "subT": np.concatenate([f32(upper[h]) for h in (2, 4, 8, 16)], 1),
        "own_u": i32(same(4) & (i < t)), "own_y": i32(same(4) & (i <= t)),
        "prev": i32(t // 4 == 2 * (u16 // 4) + 1),
    }
    for j in (1, 2, 3):
        out[f"cross{j}"] = i32(np.broadcast_to(t // 8 == j, (P, 24)))
    return {"w_" + k: v for k, v in out.items()}


def experts(nc, core, dram):
    pe, dve, act, pool, sp = core.queues
    FC, KT = F // P, CAP // P
    HALF = 512
    with ExitStack() as ctx:
        def sb(name, width, dt=F32):
            return ctx.enter_context(nc.sbuf_tensor("moe_" + name, [P, width], dt))

        w1, w2 = sb("w1", G * F), sb("w2", FC * C)
        h_rows, acc_rows, result, hT = sb("h_rows", KT * C), sb("acc_rows", KT * C), sb("result", KT * C), sb("hT", G * CAP)
        hidden = [sb(f"hidden{i}", HALF) for i in range(4)]
        ident, b1_all, b1, b2 = sb("ident", P), sb("b1_all", E * FC), sb("b1", FC), sb("b2", C)
        order = sb("order", E * KT, I32)
        slots, slots_next = sb("slots", KT, I32), sb("slots_next", KT, I32)
        banks = [ctx.enter_context(nc.psum_tensor(f"moe_bank{i}", [P, 512], F32)) for i in range(8)]

        w1v = w1[:, :].rearrange("p (g f) -> p g f", g=G)
        w1_dram = lambda e: dram["w1"][bass.ds(e, 1)].rearrange("o (g p) f -> (o p) g f", p=P)
        w2_dram = lambda e: dram["w2"][bass.ds(e, 1)].rearrange("o (k p) c -> (o p) k c", p=P)
        w2v = w2[:, :].rearrange("p (k c) -> p k c", k=FC)
        tile = lambda a, t: a[:, t * C:(t + 1) * C]

        def gather(rows, source, index, counter):
            for t in range(KT):
                pool.e.indirect_dma_start(tile(rows, t), None, source,
                                          bass.IndirectOffsetOnAxis(ap=index[:, t:t + 1], axis=0)).then_inc(counter, 16)

        core.dma(sp, "const", ident[:, :], dram["ident"])
        core.dma(sp, "const", b1_all[:, :], dram["b1"])
        with nc.allow_non_contiguous_dma(reason="one token index per partition and tile, loaded once"):
            got = core.dma(sp, "const", order[:, :], dram["order"].rearrange("(t p) o -> p (t o)", p=P))
        core.dma(sp, "weights", w1v, w1_dram(0))
        core.dma(sp, "weights", w2v, w2_dram(0))
        dve.wait(got)
        got = dve.did(dve.e.tensor_copy(slots_next[:, :], order[:, 0:KT]))
        pool.wait(got)
        gather(h_rows, dram["h"], slots_next, core.got_h)
        core.pool_sees(core.got_h, KT * 16)
        core.meet()

        def expert(e, is_last):
            new_slots = dve.did(dve.e.tensor_copy(slots[:, :], order[:, bass.ds(e * KT, KT)]))
            b1_at = dve.did(dve.e.tensor_copy(b1[:, :], b1_all[:, bass.ds(e * FC, FC)]))
            b2_at = core.dma(sp, "b2", b2[:, :], dram["b2"][bass.ds(e, 1)].to_broadcast([P, C]))
            pool.wait(new_slots)
            gather(acc_rows, dram["acc"], slots, core.got_acc)

            free = [None] * 8
            for t in range(KT):
                pe.wait(free[t])
                for g in range(G):
                    turned = pe.did(pe.e.transpose(banks[t][:, g * P:(g + 1) * P],
                                                   h_rows[:, t * C + g * P:t * C + (g + 1) * P], ident[:, :]))
                dst = hT[:, :].rearrange("p (g t) -> p g t", g=G)[:, :, t * P:(t + 1) * P]
                src = banks[t][:, :].rearrange("p (g t) -> p g t", g=G)
                if t % 2:
                    dve.wait(turned)
                    free[t] = dve.did(dve.e.tensor_copy(dst, src))
                else:
                    act.wait(turned)
                    free[t] = act.did(act.e.copy(dst, src))
            hT_at = free[KT - 2], free[KT - 1]
            if not is_last:
                more = dve.did(dve.e.tensor_copy(slots_next[:, :], order[:, bass.ds(e * KT + KT, KT)]))
                pool.wait(more, turned)
                gather(h_rows, dram["h"], slots_next, core.got_h)
            core.pool_sees(core.got_acc, e * (KT * 16) + KT * 16)
            pool.wait(b2_at)
            for t in range(KT):
                biased = pool.did(pool.e.tensor_tensor(tile(acc_rows, t), tile(acc_rows, t), b2[:, :], ALU.add))

            up, down = banks[0:4], banks[4:8]
            activated, used = {}, {}
            up_free, down_free = [free[i] for i in range(4)], [free[4 + i] for i in range(4)]
            steps = [(half, k) for half in range(2) for k in range(FC)]
            drained = []

            def widen(at):
                half, k = steps[at]
                bank = up[at % 4]
                pe.wait(up_free[at % 4], *hT_at)
                for g in range(G):
                    mm = pe.e.matmul(bank[:, :], w1[:, g * F + k * P:g * F + (k + 1) * P],
                                     hT[:, g * CAP + half * HALF:g * CAP + (half + 1) * HALF],
                                     start=g == 0, stop=g == G - 1)
                act.wait(pe.did(mm), used.get(at - 4), b1_at)
                activated[at] = up_free[at % 4] = act.did(act.e.activation(
                    hidden[at % 4][:, :], bank[:, :], ACT.Gelu_apprx_tanh, bias=b1[:, k:k + 1]))

            def narrow(at):
                half, k = steps[at]
                pe.wait(activated[at])
                for t in range(4):
                    if k == 0:
                        pe.wait(down_free[t])
                    mm = pe.e.matmul(down[t][:, :], hidden[at % 4][:, t * P:(t + 1) * P], tile(w2, k),
                                     start=k == 0, stop=k == FC - 1)
                used[at] = pe.did(mm)
                if half == 1 and not is_last and k % 4 == 3:
                    sp.wait(used[at])
                    lo = k - 3
                    core.dma(sp, "weights", w1v[:, :, lo * P:(k + 1) * P], w1_dram(e + 1)[:, :, lo * P:(k + 1) * P])
                    core.dma(sp, "weights", w2v[:, lo:k + 1], w2_dram(e + 1)[:, lo:k + 1])
                if k == FC - 1:
                    dve.wait(used[at], biased)
                    for t in range(4):
                        down_free[t] = dve.did(dve.e.tensor_tensor(
                            tile(result, half * 4 + t), down[t][:, :], tile(acc_rows, half * 4 + t), ALU.add))
                        pool.wait(down_free[t])
                        pool.e.indirect_dma_start(
                            dram["out"], bass.IndirectOffsetOnAxis(ap=slots[:, half * 4 + t:half * 4 + t + 1], axis=0),
                            tile(result, half * 4 + t), None).then_inc(core.stored, 16)

            widen(0)
            for at in range(len(steps)):
                if at + 1 < len(steps):
                    widen(at + 1)
                narrow(at)
            core.pool_sees(core.stored, e * (KT * 16) + KT * 16)
            if not is_last:
                core.pool_sees(core.got_h, e * (KT * 16) + 2 * KT * 16)
            core.meet()

        with nc.Fori(0, E - 1) as e:
            expert(e, False)
        expert(E - 1, True)


def mixer_with_experts(nc, dram):
    with ExitStack() as ctx:
        core = Core(nc, ctx)
        norm_and_scores(nc, core, dram)
        route(nc, core, dram)
        time_mix(nc, core, dram)
        experts(nc, core, dram)


def kernel(**inputs):
    import concourse.bacc as bacc
    from concourse.bass_utils import run_bass_kernel_spmd

    attn = {k[len("L0_attn_"):]: np.asarray(v) for k, v in inputs.items() if k.startswith("L0_attn_")}
    ffn = {k[len("L0_ffn_"):]: np.asarray(v) for k, v in inputs.items() if k.startswith("L0_ffn_")}
    arrays = {
        "x": attn["x"].reshape(NT, C),
        "ln_g": ffn["ln_g"].reshape(1, C), "ln_b": ffn["ln_b"].reshape(1, C),
        "centT": ffn["centroids"].T.reshape(G, P, E).transpose(1, 0, 2),
        "w1": ffn["w1"], "w2": ffn["w2"], "b2": ffn["b2"],
        "b1": ffn["b1"].reshape(E * F // P, P).T,
        "ident": np.eye(P, dtype=np.float32), "ones": np.ones((P, P), np.float32),
        "before": np.triu(np.ones((P, P), np.float32), 1),
        "steps15": np.tile(np.arange(1, 16, dtype=np.float32), (P, 1)),
        **time_mix_inputs(attn),
    }
    arrays = {k: np.ascontiguousarray(a) for k, a in arrays.items()}
    nc = bacc.Bacc("TRN2", target_bir_lowering=False, num_devices=1)
    dram = {k: nc.dram_tensor("in_" + k, a.shape, mybir.dt.from_np(a.dtype), kind="ExternalInput").ap()
            for k, a in arrays.items()}
    for name, shape, dt in (("xn", (NT, C), F32), ("h", (NT, C), F32), ("scores", (NT, E), F32),
                            ("order", (NT, 1), I32), ("acc", (NT, C), F32)):
        dram[name] = nc.dram_tensor("mid_" + name, shape, dt, kind="Internal").ap()
    dram["out"] = nc.dram_tensor("out", (NT, C), F32, kind="ExternalOutput").ap()
    mixer_with_experts(nc, dram)
    r = run_bass_kernel_spmd(nc, [{"in_" + k: a for k, a in arrays.items()}], core_ids=[0])
    return r.results[0]["out"].reshape(B, T, C)
```

```python
import numpy as np
import concourse.bass as bass
from concourse import mybir
from contextlib import ExitStack

F32, I32 = mybir.dt.float32, mybir.dt.int32
ALU, ACT, AX = mybir.AluOpType, mybir.ActivationFunctionType, mybir.AxisListType

P = 128
B, T, C = 2, 4096, 512
NT = B * T
G = C // P
N = 32
HG = P // N
E, F = 8, 2048
CAP = NT // E
EPS = 1e-5


class Queue:

    def __init__(self, engine, sem):
        self.e, self.sem, self.n, self.seen = engine, sem, 0, {}

    def did(self, instruction):
        instruction.then_inc(self.sem, 1)
        self.n += 1
        return self.sem, self.n

    def wait(self, *steps):
        for step in steps:
            if step is not None and self.seen.get(step[0].name, 0) < step[1]:
                self.seen[step[0].name] = step[1]
                self.e.wait_ge(*step)


class Core:

    def __init__(self, nc, ctx):
        self.nc, self.ctx, self.streams, self.counts = nc, ctx, {}, {}
        queue = lambda e, name: Queue(e, ctx.enter_context(nc.semaphore(name)))
        self.pe, self.dve = queue(nc.tensor, "pe_steps"), queue(nc.vector, "dve_steps")
        self.act, self.pool = queue(nc.scalar, "act_steps"), queue(nc.gpsimd, "pool_steps")
        self.sp = queue(nc.sync, "sp_steps")
        self.scattered, self.got_h, self.got_acc, self.stored = (
            ctx.enter_context(nc.semaphore(n)) for n in ("scattered", "got_h", "got_acc", "stored"))
        self.tick = ctx.enter_context(nc.sbuf_tensor("tick", [P, 1], F32))
        nc.gpsimd.memset(self.tick[:, :], 0.0).then_inc(self.pool.sem, 1)
        self.pool.n = 1
        self.queues = (self.pe, self.dve, self.act, self.pool, self.sp)

    def dma(self, queue, stream, out, in_):
        return self.landed(stream, queue.e.dma_start(out, in_))

    def landed(self, stream, instruction):
        if stream not in self.streams:
            self.streams[stream] = self.ctx.enter_context(self.nc.semaphore("dma_" + stream))
            self.counts[stream] = 0
        self.counts[stream] += 16
        instruction.then_inc(self.streams[stream], 16)
        return self.streams[stream], self.counts[stream]

    def pool_sees(self, counter, value):
        pool = self.pool
        pool.e.wait_ge(pool.sem, pool.n)
        pool.e.wait_ge(counter, value)
        return pool.did(pool.e.tensor_tensor(self.tick[:, :], self.tick[:, :], self.tick[:, :], ALU.add))

    def meet(self):
        for name, count in self.counts.items():
            if count:
                self.sp.wait((self.streams[name], count))
        for q in self.queues:
            if q.n:
                q.e.wait_ge(q.sem, q.n)
        self.nc.all_engine_barrier()
        for q in self.queues:
            if q.n:
                self.nc.sync.sem_clear(q.sem)
        for name, count in self.counts.items():
            if count:
                self.nc.sync.sem_clear(self.streams[name])
        self.nc.all_engine_barrier()
        for q in self.queues:
            q.n, q.seen = 0, {}
        self.counts = dict.fromkeys(self.counts, 0)


def norm_and_scores(nc, core, dram):
    pe, dve, act, pool, sp = core.queues
    SUB = 8
    with ExitStack() as ctx:
        sb = lambda name, shape, dt=F32: ctx.enter_context(nc.sbuf_tensor(name, shape, dt))
        x, xn, h0, h, hT = (sb(f"a_{n}", [P, SUB, C]) for n in ("x", "xn", "h0", "h", "hT"))
        gain, bias, cent = sb("a_gain", [P, C]), sb("a_bias", [P, C]), sb("a_cent", [P, G, E])
        ident = sb("a_ident", [P, P])
        stats, mv, var, std, rstd = (sb(f"a_{n}", [P, 2, SUB, k]) for n, k in (
            ("stats", 6), ("mv", 2), ("var", 1), ("std", 1), ("rstd", 1)))
        scores = sb("a_scores", [P, SUB, E])
        turn = [ctx.enter_context(nc.psum_tensor(f"a_turn{i}", [P, C], F32)) for i in range(2)]
        score_ps = ctx.enter_context(nc.psum_tensor("a_score_ps", [P, SUB, E], F32))
        core.dma(sp, "const", gain[:, :], dram["ln_g"].to_broadcast([P, C]))
        core.dma(sp, "const", bias[:, :], dram["ln_b"].to_broadcast([P, C]))
        core.dma(sp, "const", cent[:, :, :], dram["centT"])
        core.dma(sp, "const", ident[:, :], dram["ident"])
        core.meet()
        rows = lambda a, i: a.rearrange("(i s p) c -> i p s c", s=SUB, p=P)[bass.ds(i, 1)].rearrange(
            "o p s c -> (o p) s c")
        with nc.Fori(0, NT // (SUB * P)) as i:
            x_in = core.dma(sp, "x", x[:, :, :], rows(dram["x"], i))

            def normalise(which, src, dst, ready):
                dve.wait(ready)
                for s in range(SUB):
                    got = dve.did(dve.e.bn_stats(stats[:, which, s], src[:, s]))
                dve.wait(got)
                for s in range(SUB):
                    got = dve.did(dve.e.bn_aggr(mv[:, which, s], stats[:, which, s]))
                dve.wait(got)
                got = dve.did(dve.e.tensor_scalar(var[:, which, :, 0], mv[:, which, :, 1], EPS, None, ALU.add))
                act.wait(got)
                got = act.did(act.e.activation(std[:, which, :, 0], var[:, which, :, 0], ACT.Sqrt))
                dve.wait(got)
                got = dve.did(dve.e.reciprocal(rstd[:, which, :, 0], std[:, which, :, 0]))
                dve.wait(got)
                for s in range(SUB):
                    got = dve.did(dve.e.tensor_scalar(dst[:, s], src[:, s], mv[:, which, s, 0:1],
                                                      rstd[:, which, s], ALU.subtract, ALU.mult))
                return got

            xn_done = normalise(0, x, xn, x_in)
            sp.wait(xn_done)
            core.dma(sp, "xn", rows(dram["xn"], i), xn[:, :, :])
            h0_done = normalise(1, xn, h0, xn_done)
            dve.wait(h0_done)
            bc = lambda a: a[:, :].rearrange("p (s c) -> p s c", s=1).to_broadcast([P, SUB, C])
            gained = dve.did(dve.e.tensor_tensor(h0[:, :, :], h0[:, :, :], bc(gain), ALU.mult))
            dve.wait(gained)
            h_done = dve.did(dve.e.tensor_tensor(h[:, :, :], h0[:, :, :], bc(bias), ALU.add))
            sp.wait(h_done)
            core.dma(sp, "h", rows(dram["h"], i), h[:, :, :])
            pe.wait(h_done)
            copied = {}
            for s in range(SUB):
                pe.wait(copied.get(s - 2))
                for g in range(G):
                    turned = pe.did(pe.e.transpose(turn[s % 2][:, g * P:(g + 1) * P],
                                                   h[:, s, g * P:(g + 1) * P], ident[:, :]))
                act.wait(turned)
                copied[s] = act.did(act.e.copy(hT[:, s], turn[s % 2][:, :]))
            for s in range(SUB):
                pe.wait(copied[s])
                for g in range(G):
                    mm = pe.e.matmul(score_ps[:, s], hT[:, s, g * P:(g + 1) * P], cent[:, g],
                                     start=g == 0, stop=g == G - 1)
            scored = pe.did(mm)
            dve.wait(scored)
            out = dve.did(dve.e.tensor_copy(scores[:, :, :], score_ps[:, :, :]))
            sp.wait(out)
            core.dma(sp, "scores", dram["scores"].rearrange("(i s p) e -> i p s e", s=SUB, p=P)[
                bass.ds(i, 1)].rearrange("o p s e -> (o p) s e"), scores[:, :, :])
            core.meet()


def route(nc, core, dram):
    pe, dve, act, pool, sp = core.queues
    TT = NT // P
    J = 15
    with ExitStack() as ctx:
        sb = lambda name, shape, dt=F32: ctx.enter_context(nc.sbuf_tensor(name, shape, dt))
        score = sb("r_score", [P, TT, E])
        sign, key, part = (sb(f"r_{n}", [P, TT, E], I32) for n in ("sign", "key", "part"))
        hi, lo = sb("r_hi", [P, E, TT]), sb("r_lo", [P, E, TT])
        free, slot, hi_e, lo_e = (sb(f"r_{n}", [P, TT]) for n in ("free", "slot", "hi_e", "lo_e"))
        above, equal, tie, rank, scan, tmp = (sb(f"r_{n}", [P, TT]) for n in (
            "above", "equal", "tie", "rank", "scan", "tmp"))
        ge, cand, cnt, steps15 = sb("r_ge", [P, J, TT]), sb("r_cand", [P, J]), sb("r_cnt", [P, J]), sb("r_15", [P, J])
        cur_hi, cur_lo, nsel, need, base, ones1 = (sb(f"r_{n}", [P, 1]) for n in (
            "cur_hi", "cur_lo", "nsel", "need", "base", "ones1"))
        junk = sb("r_junk", [P, J])
        onesT = sb("r_onesT", [P, TT])
        ones, before = sb("r_ones", [P, P]), sb("r_before", [P, P])
        slot_i, ids, slot8, ids8 = (sb(f"r_{n}", s, I32) for n, s in (
            ("slot_i", [P, TT]), ("ids", [P, TT]), ("slot8", [P, 8]), ("ids8", [P, 8])))
        ps = ctx.enter_context(nc.psum_tensor("r_ps", [P, 2, TT], F32))
        cps = ctx.enter_context(nc.psum_tensor("r_cps", [P, J], F32))

        def step(q, instruction):
            done = q.did(instruction)
            q.wait(done)
            return done

        core.dma(sp, "const", score[:, :, :], dram["scores"].rearrange("(t p) e -> p t e", p=P))
        core.dma(sp, "const", ones[:, :], dram["ones"])
        core.dma(sp, "const", before[:, :], dram["before"])
        core.dma(sp, "const", steps15[:, :], dram["steps15"])
        step(pool, pool.e.iota(ids[:, :], pattern=[[P, TT]], base=0, channel_multiplier=1))
        for a, v in ((free, 1.0), (slot, 0.0), (base, 0.0), (ones1, 1.0), (onesT, 1.0)):
            step(dve, dve.e.memset(a[:, :], v))
        core.meet()
        bits = score[:, :, :].bitcast(I32)
        step(dve, dve.e.tensor_scalar(sign[:, :, :], bits, 31, -2147483648, ALU.arith_shift_right, ALU.bitwise_or))
        step(dve, dve.e.tensor_tensor(key[:, :, :], bits, sign[:, :, :], ALU.bitwise_xor))
        step(dve, dve.e.tensor_scalar(part[:, :, :], key[:, :, :], 16, None, ALU.logical_shift_right))
        step(dve, dve.e.tensor_copy(hi[:, :, :].rearrange("p e t -> p t e"), part[:, :, :]))
        step(dve, dve.e.tensor_scalar(part[:, :, :], key[:, :, :], 65535, None, ALU.bitwise_and))
        step(dve, dve.e.tensor_copy(lo[:, :, :].rearrange("p e t -> p t e"), part[:, :, :]))
        core.meet()

        def total(mask, out):
            step(dve, dve.e.tensor_reduce(cnt[:, 0:1], mask[:, :], AX.X, ALU.add))
            pe.wait((dve.sem, dve.n))
            got = pe.did(pe.e.matmul(cps[:, 0:1], ones[:, :], cnt[:, 0:1], start=True, stop=True))
            dve.wait(got)
            step(dve, dve.e.tensor_copy(out[:, :], cps[:, 0:1]))

        def search(values, wanted, cur):
            step(dve, dve.e.memset(cur[:, :], 0.0))
            for bit in (12, 8, 4, 0):
                size = float(1 << bit)
                step(dve, dve.e.tensor_scalar(cand[:, :], steps15[:, :], size, cur[:, 0:1], ALU.mult, ALU.add))
                step(dve, dve.e.tensor_tensor(
                    ge[:, :, :], values[:, :].rearrange("p (j t) -> p j t", j=1).to_broadcast([P, J, TT]),
                    cand[:, :].rearrange("p (j t) -> p j t", t=1).to_broadcast([P, J, TT]), ALU.is_ge))
                step(dve, dve.e.tensor_reduce(cnt[:, :], ge[:, :, :], AX.X, ALU.add))
                pe.wait((dve.sem, dve.n))
                got = pe.did(pe.e.matmul(cps[:, :], ones[:, :], cnt[:, :], start=True, stop=True))
                dve.wait(got)
                step(dve, dve.e.tensor_scalar(junk[:, :], cps[:, :], wanted, None, ALU.is_ge, ALU.add,
                                              accum_out=nsel[:, :]))
                step(dve, dve.e.scalar_tensor_tensor(cur[:, :], nsel[:, :], size, cur[:, :], ALU.mult, ALU.add))

        def ranks(mask):
            pe.wait((dve.sem, dve.n))
            pe.e.matmul(ps[:, 0], before[:, :], mask[:, :], start=True, stop=True)
            got = pe.did(pe.e.matmul(ps[:, 1], ones[:, :], mask[:, :], start=True, stop=True))
            dve.wait(got)
            step(dve, dve.e.tensor_copy(tmp[:, :], ps[:, 1]))
            step(dve, dve.e.tensor_tensor_scan(scan[:, :], onesT[:, :], tmp[:, :], 0.0, ALU.mult, ALU.add))
            step(dve, dve.e.tensor_tensor(scan[:, :], scan[:, :], tmp[:, :], ALU.subtract))
            step(dve, dve.e.tensor_tensor(rank[:, :], ps[:, 0], scan[:, :], ALU.add))

        def masked(out, values, mask):
            step(dve, dve.e.scalar_tensor_tensor(out[:, :], values, 1.0, mask[:, :], ALU.add, ALU.mult))
            step(dve, dve.e.tensor_scalar(out[:, :], out[:, :], -1.0, None, ALU.add))

        with nc.Fori(0, E) as e:
            masked(hi_e, hi[:, bass.ds(e, 1), :].rearrange("p o t -> p (o t)"), free)
            search(hi_e, float(CAP), cur_hi)
            step(dve, dve.e.tensor_scalar(above[:, :], hi_e[:, :], cur_hi[:, 0:1], None, ALU.is_gt))
            step(dve, dve.e.tensor_scalar(equal[:, :], hi_e[:, :], cur_hi[:, 0:1], None, ALU.is_equal))
            total(above, need)
            step(dve, dve.e.tensor_scalar(need[:, :], need[:, :], -1.0, float(CAP), ALU.mult, ALU.add))
            masked(lo_e, lo[:, bass.ds(e, 1), :].rearrange("p o t -> p (o t)"), equal)
            search(lo_e, need[:, 0:1], cur_lo)
            step(dve, dve.e.tensor_scalar(tmp[:, :], lo_e[:, :], cur_lo[:, 0:1], None, ALU.is_gt))
            step(dve, dve.e.tensor_tensor(above[:, :], above[:, :], tmp[:, :], ALU.add))
            step(dve, dve.e.tensor_scalar(tie[:, :], lo_e[:, :], cur_lo[:, 0:1], None, ALU.is_equal))
            total(above, need)
            step(dve, dve.e.tensor_scalar(need[:, :], need[:, :], -1.0, float(CAP), ALU.mult, ALU.add))
            ranks(tie)
            step(dve, dve.e.scalar_tensor_tensor(tie[:, :], rank[:, :], need[:, 0:1], tie[:, :], ALU.is_lt, ALU.mult))
            step(dve, dve.e.tensor_tensor(above[:, :], above[:, :], tie[:, :], ALU.add))
            ranks(above)
            step(dve, dve.e.scalar_tensor_tensor(tmp[:, :], rank[:, :], base[:, 0:1], above[:, :], ALU.add, ALU.mult))
            step(dve, dve.e.tensor_tensor(slot[:, :], slot[:, :], tmp[:, :], ALU.add))
            step(dve, dve.e.tensor_tensor(free[:, :], free[:, :], above[:, :], ALU.subtract))
            step(dve, dve.e.tensor_scalar(base[:, :], base[:, :], float(CAP), None, ALU.add))
            core.meet()
        step(dve, dve.e.tensor_copy(slot_i[:, :], slot[:, :]))
        core.meet()
        with nc.Fori(0, TT // 8) as i:
            dve.did(dve.e.tensor_copy(slot8[:, :], slot_i[:, bass.ds(i * 8, 8)]))
            got = dve.did(dve.e.tensor_copy(ids8[:, :], ids[:, bass.ds(i * 8, 8)]))
            pool.wait(got)
            for j in range(8):
                pool.e.indirect_dma_start(
                    dram["order"], bass.IndirectOffsetOnAxis(ap=slot8[:, j:j + 1], axis=0),
                    ids8[:, j:j + 1], None).then_inc(core.scattered, 16)
            core.pool_sees(core.scattered, i * 128 + 128)
            core.meet()
TB = P // B
NC = TB // N
U = G * B * NC
SU = G * B
W4, W8 = N + N // 2, 6 * 8
FLOOR = -19.5


def time_mix(nc, core, dram):
    pe, dve, act, pool, sp = core.queues
    with ExitStack() as ctx:
        def sb(name, width=G * P, dt=F32):
            return ctx.enter_context(nc.sbuf_tensor("time_" + name, [P, width], dt))

        wt = {}
        for name in ("receptance", "key_w", "value", "output"):
            wt[name] = sb(name, G * C)
        wt["maa_w2"] = sb("maa_w2", 4 * C)
        for name in ("maa_w1", "gate_w1", "gate_w2", "low_wa", "low_k",
                     "decay_w2", "mk_aaa_w2", "kkk_ma_w2"):
            wt[name] = sb(name, C)
        for name, width in (("ident", P), ("head_ones", P), ("eye", N), ("one_wa", 1), ("minus_half", 1), ("one_k", 1),
                            ("maa_x", G), ("maa", 4 * G), ("faaaa", G), ("ln_w", G), ("ln_b", G),
                            ("restart", G * P), ("pair_u", N), ("pair_uT", N), ("subT", 4 * N)):
            wt[name] = sb(name, width)
        for name, width in (("own_u", N), ("own_y", N), ("prev", 16), ("cross1", 24),
                            ("cross2", 24), ("cross3", 24)):
            wt[name] = sb(name, width, I32)
        for name, tensor in wt.items():
            core.dma(sp, "const", tensor[:, :], dram["w_" + name])

        handed = [{n: sb(f"{n}_{s}", width) for n, width in (
            ("base", C), ("gate", G * P), ("bonus_v", G * P), ("ys", G * P), ("us", G * P),
            ("kT", G * P), ("bT", G * P), ("vT", G * P), ("inv", G * P), ("invT", G * P),
            ("aT_u", U * 2 * N), ("aT_y", U * 2 * N), ("decay_end", U))} for s in range(2)]
        third = lambda t, i: t[:, i * G * P:(i + 1) * G * P]
        xn_rows, x_rows = sb("xn_rows"), sb("x_rows")
        x = sb("x", G * B * (TB + 1))
        xx, lerp, mix = sb("xx"), sb("lerp"), sb("mix", P)
        xxx = lerp
        xf_all, trio = sb("xf", 4 * G * P), sb("trio", 3 * G * P)
        xf = [third(xf_all, f) for f in range(4)]
        hid_g, hid_wa, hid_k = mix, sb("hid_wa", P), sb("hid_k", P)
        zc, w, a = (third(trio, f) for f in range(3))
        k, soft, ma, mk, sq = (sb(n) for n in ("k", "soft", "ma", "mk", "sq"))
        wc = soft
        size = sb("size", U)
        minus_half = wt["minus_half"][:, 0:1].to_broadcast([P, U])
        r, kk, k2, b, v, csum, cprev = (sb(n) for n in ("r", "kk", "k2", "b", "v", "csum", "cprev"))
        key4, key8 = xf_all[:, 0:U * 2 * W4], trio[:, 0:U * 2 * W8]
        diff, grow = [xf[3], xx], [lerp, sq]
        k_end, b_end = ma, mk
        q = {"y4": k, "u4": soft, "y8": v}
        wide_q = {n: sb("wide_" + n, U * P) for n in ("u4", "y4", "u8")}
        wide_q["y8"] = wide_q["u4"]
        a_u, a_y = sb("a_u", U * 2 * N), sb("a_y", U * 2 * N)
        sub, part, invT1 = sb("sub"), sb("part"), sb("invT1")
        rhs, corr = part[:, 0:SU * N], part[:, SU * N:2 * SU * N]
        y, squares, acc, mixed = invT1, sub, sub, part
        state, faded = sb("state", SU * N), sub[:, 0:SU * N]
        mean, var = sb("mean", U), sb("var", U)

        banks = [ctx.enter_context(nc.psum_tensor(f"w_bank{i}", [P, 512], F32)) for i in range(8)]
        last_read = [None] * 8
        taken = {"front": 0, "back": 0}
        own_banks = {"front": (0, 1, 2, 3), "back": (4, 5, 6, 7)}

        def bank(who="front"):
            i = own_banks[who][taken[who] % len(own_banks[who])]
            taken[who] += 1
            pe.wait(last_read[i])
            return i, banks[i]

        def tt(qu, out, in0, in1, op, *needs):
            qu.wait(*needs)
            return qu.did(qu.e.tensor_tensor(out, in0, in1, op))

        def ts(qu, out, in0, s0, s1, op0, op1, *needs):
            qu.wait(*needs)
            return qu.did(qu.e.tensor_scalar(out, in0, s0, s1, op0, op1) if s1 is not None
                          else qu.e.tensor_scalar(out, in0, s0, None, op0))

        def stt(out, in0, s, in1, op0, op1, *needs):
            dve.wait(*needs)
            return dve.did(dve.e.scalar_tensor_tensor(out, in0, s, in1, op0, op1))

        def fn(out, in_, func, *needs, bias=0.0, scale=1.0):
            act.wait(*needs)
            return act.did(act.e.activation(out, in_, func, bias=bias, scale=scale))

        def copy(out, in_, *needs):
            act.wait(*needs)
            return act.did(act.e.copy(out, in_))

        def turn(out, in_, *needs):
            dve.wait(*needs)
            return dve.did(dve.e.transpose(out, in_))

        def project(weight, width, columns, rhs_of, *needs, steps=G, rows=slice(0, P)):
            i, ps = bank()
            pe.wait(*needs)
            for o in range(len(columns)):
                for g in range(steps):
                    mm = pe.e.matmul(ps[:, o * P:(o + 1) * P],
                                     weight[rows, g * width + columns[o]:g * width + columns[o] + P],
                                     rhs_of(g), start=g == 0, stop=g == steps - 1)
                if steps > 1 and o + 1 < len(columns):
                    yield
            return i, ps, pe.did(mm)

        full = [g * P for g in range(G)]
        col = lambda t: t[:, :]
        grp = lambda t, g: t[:, g * P:(g + 1) * P]
        chunks = lambda t: t[:, :].rearrange("p (n t) -> p n t", t=N)
        fours = lambda t: t[:, :].rearrange("p (q t) -> p q t", t=4)
        eights = lambda t: t[:, :].rearrange("p (q t) -> p q t", t=8)
        per_group = lambda t: t[:, :].rearrange("p (g o) -> p g o", o=1).to_broadcast([P, G, P])
        groups = lambda t: t[:, :].rearrange("p (g c) -> p g c", c=P)
        head = lambda h: slice(h * N, (h + 1) * N)
        blk = lambda n: slice(n * N, (n + 1) * N)

        for t in (x, a_u, a_y, state, hid_k, *(wide_q[n] for n in ("u4", "y4", "u8"))):
            dve.did(dve.e.memset(t[:, :], 0.0))
        core.meet()
        xs = x[:, :].rearrange("p (g b t) -> p g b t", g=G, b=B)
        xnow = xs[:, :, :, 1:TB + 1]
        by_b = lambda t: t[:, :].rearrange("p (g b t) -> p g b t", g=G, b=B)
        tile_rows = lambda a, i, s: a.rearrange("(b i t) c -> b i t c", b=B, t=TB)[s][bass.ds(i, 1)].rearrange(
            "o t c -> (o t) c")

        def load_rows(i):
            for s in range(B):
                half = slice(s * TB, (s + 1) * TB)
                core.dma(sp, "w_xn", xn_rows[half, :], tile_rows(dram["xn"], i, s))
                core.dma(sp, "w_x", x_rows[half, :], tile_rows(dram["x"], i, s))

        def front(i, out, follows):
            base, gate, bonus, aT_u, aT_y, decay_end = (out[n] for n in (
                "base", "gate", "bonus_v", "aT_u", "aT_y", "decay_end"))
            inv, invT = out["inv"], out["invT"]
            q["u8"] = aT_y[:, 0:G * P]
            based = tt(pool, col(base), col(x_rows), col(xn_rows), ALU.add)
            yield
            bi, ps = bank()
            for g in range(G):
                turned = pe.did(pe.e.transpose(ps[:, g * P:(g + 1) * P], grp(xn_rows, g), wt["ident"][:, :]))
            carried = copy(xs[:, :, :, 0:1], xs[:, :, :, TB:TB + 1])
            if follows is not None:
                sp.wait(turned, based)
                load_rows(follows)
            x_at = last_read[bi] = copy(xnow, by_b(ps), turned, carried)
            yield
            xx_at = tt(dve, by_b(xx), xs[:, :, :, 0:TB], xnow, ALU.subtract, x_at)
            dve.wait(xx_at)
            for g in range(G):
                xxx_at = stt(grp(xxx, g).rearrange("p (b t) -> p b t", b=B),
                             grp(xx, g).rearrange("p (b t) -> p b t", b=B), wt["maa_x"][:, g:g + 1],
                             xs[:, g, :, 1:TB + 1], ALU.mult, ALU.add)
            yield
            bi, ps, done = yield from project(wt["maa_w1"], P, [0], lambda g: grp(xxx, g), xxx_at)
            mix_at = last_read[bi] = fn(col(mix), ps[:, 0:P], ACT.Tanh, done)
            xf_at = []
            added = None
            for f in range(4):
                bi, ps, done = yield from project(wt["maa_w2"], 0, [f * C + g * P for g in range(G)],
                                       lambda g: col(mix), mix_at, steps=1)
                dve.wait(done, added)
                for g in range(G):
                    lerped = stt(grp(lerp, g), grp(ps, g), wt["maa"][:, f * G + g:f * G + g + 1],
                                 grp(xx, g), ALU.add, ALU.mult)
                last_read[bi] = lerped
                added = tt(dve, by_b(xf[f]), by_b(lerp), xnow, ALU.add, lerped)
                xf_at.append(added)
                yield

            yield
            bi, ps, done = yield from project(wt["low_wa"], P, [0], lambda g: grp(xf[1], g), xf_at[1])
            wa0 = fn(hid_wa[0:64, :], ps[0:64, 0:P], ACT.Tanh, done)
            wa_at = last_read[bi] = fn(hid_wa[64:P, :], ps[64:P, 0:P], ACT.Identity, bias=wt["one_wa"][64:P, 0:1])
            yield
            bi, ps, done = yield from project(wt["low_k"], P, [0], lambda g: grp(xf[2], g), xf_at[2])
            fn(hid_k[0:32, :], ps[0:32, 0:P], ACT.Tanh, done)
            hk_at = last_read[bi] = fn(hid_k[32:64, :], ps[32:64, 0:P], ACT.Identity, bias=wt["one_k"][32:64, 0:1])
            yield
            bi, ps, done = yield from project(wt["gate_w1"], P, [0], lambda g: grp(xf[0], g), xf_at[0])
            hg_at = last_read[bi] = fn(col(hid_g), ps[:, 0:P], ACT.Tanh, done)
            yield
            bi, ps, done = yield from project(wt["decay_w2"], 0, full, lambda g: col(hid_wa), wa_at, wa0, steps=1)
            z = ps
            zc_at = ts(dve, col(zc), col(z), FLOOR, None, ALU.max, None, done)
            below_at = last_read[bi] = tt(dve, col(w), col(z), col(zc), ALU.subtract, zc_at)
            yield
            bi, ps, done = yield from project(wt["key_w"], C, full, lambda g: grp(xf[2], g))
            k_at = last_read[bi] = copy(col(k), col(ps), done)
            yield
            bi, ps, done = yield from project(wt["kkk_ma_w2"], 0, full, lambda g: col(hid_k), hk_at, steps=1)
            kkr_at = last_read[bi] = tt(dve, col(kk), col(ps), col(k), ALU.add, done, k_at)
            kkT_at = turn(col(sq), col(kk), kkr_at)
            yield
            bi, ps, done = yield from project(wt["mk_aaa_w2"], 0, full, lambda g: hid_wa[64:P, :], steps=1, rows=slice(64, P))
            th_a = last_read[bi] = fn(col(a), col(ps), ACT.Tanh, done, scale=0.5)
            yield
            bi, ps, done = yield from project(wt["kkk_ma_w2"], 0, full, lambda g: hid_wa[64:P, :], steps=1, rows=slice(64, P))
            th_ma = last_read[bi] = fn(col(ma), col(ps), ACT.Tanh, done, scale=0.5)
            yield
            bi, ps, done = yield from project(wt["mk_aaa_w2"], 0, full, lambda g: col(hid_k), steps=1)
            th_mk = last_read[bi] = fn(col(mk), col(ps), ACT.Tanh, done, scale=0.5)
            soft_at = fn(col(soft), col(zc), ACT.Exp, zc_at, scale=-1.0)
            yield
            bi, ps, done = yield from project(wt["receptance"], C, full, lambda g: grp(xf[0], g))
            r_at = last_read[bi] = copy(col(r), col(ps), done)
            yield
            bi, ps, done = yield from project(wt["value"], C, full, lambda g: grp(xf[3], g), xf_at[3])
            v_at = last_read[bi] = copy(col(v), col(ps), done)
            yield
            bi, ps, done = yield from project(wt["gate_w2"], 0, full, lambda g: col(hid_g), hg_at, steps=1)
            projected = done
            gate_at = last_read[bi] = copy(col(gate), col(ps), done)
            yield
            soft_at = fn(col(soft), col(soft), ACT.Ln, soft_at, bias=1.0)
            wc_at = ts(dve, col(wc), col(soft), -1.0, -0.5, ALU.mult, ALU.add, soft_at)
            w_at = tt(pool, col(w), col(w), col(wc), ALU.add, wc_at, below_at)
            dve.wait(wc_at)
            c_at = dve.did(dve.e.tensor_tensor_scan(col(csum), wt["restart"][:, :], col(wc), 0.0, ALU.mult, ALU.add))
            cp_at = tt(dve, col(cprev), col(csum), col(wc), ALU.subtract, c_at)
            yield
            squared = fn(col(lerp), col(sq), ACT.Square, kkT_at, added)
            dve.wait(squared)
            n0 = dve.did(dve.e.tensor_reduce(size[:, :], chunks(lerp), AX.X, ALU.add))
            n0 = ts(dve, size[:, :], size[:, :], 1e-24, None, ALU.max, None, n0)
            n1 = tt(pool, size[:, :], size[:, :], minus_half, ALU.pow, n0)
            yield
            a_at = ts(dve, col(a), col(a), 0.5, 0.5, ALU.mult, ALU.add, th_a)
            ma_at = ts(dve, col(ma), col(ma), 0.5, 0.5, ALU.mult, ALU.add, th_ma)
            mk_at = ts(pool, col(mk), col(mk), 0.5, 0.5, ALU.mult, ALU.add, th_mk)
            wmk_at = tt(pool, col(w), col(w), col(mk), ALU.mult, mk_at, w_at)
            ewmk = fn(col(w), col(w), ACT.Exp, wmk_at)
            yield
            n2 = tt(dve, chunks(sq), chunks(sq),
                    size[:, :].rearrange("p (n o) -> p n o", o=1).to_broadcast([P, U, N]), ALU.mult, n1)
            kk_at = turn(col(kk), col(sq), n2)
            yield
            t0 = stt(col(lerp), col(ma), 1.0, col(a), ALU.subtract, ALU.mult, a_at, ma_at, added)
            t1 = tt(dve, col(lerp), col(ma), col(lerp), ALU.subtract, t0)
            t2 = tt(dve, col(lerp), col(lerp), col(k), ALU.mult, t1)
            k2_at = tt(dve, col(k2), col(lerp), col(w), ALU.mult, t2, ewmk)
            yield
            b_at = stt(col(b), col(kk), -1.0, col(a), ALU.mult, ALU.mult, kk_at)
            rk = tt(pool, col(bonus), col(r), col(k2), ALU.mult, r_at, k2_at)
            rk = tt(pool, groups(bonus), groups(bonus), per_group(wt["faaaa"]), ALU.mult, rk)
            bi, ps = bank()
            pe.wait(rk)
            done = pe.did(pe.e.matmul(ps[:, :], wt["head_ones"][:, :], col(bonus), start=True, stop=True))
            bonus_at = last_read[bi] = tt(dve, col(bonus), col(ps), col(v), ALU.mult, done, v_at)
            yield
            for engine in (dve, act, pool):
                engine.wait(projected, b_at, bonus_at, kk_at, r_at, v_at, cp_at, c_at)
            vT_at = turn(col(out["vT"]), col(v))
            mid4 = fours(csum)[:, :, 1:2].to_broadcast([P, G * P // 4, 4])
            first8 = eights(cprev)[:, :, 0:1].to_broadcast([P, G * P // 8, 8])
            diff_read, grow_read = [None, None], [None, None]
            use, waiting = [0], []

            def flush():
                if waiting:
                    i, readers, e = waiting.pop()
                    grow_read[i] = readers(grow[i], e)

            def grown(shape, view, in0, in1, needs, readers, scale=1.0):
                i = use[0] % 2
                use[0] += 1
                d = tt(dve, view(diff[i]), in0, in1, ALU.subtract, diff_read[i], *needs)
                diff_read[i] = e = fn(shape(grow[i]), shape(diff[i]), ACT.Exp, d, grow_read[i], scale=scale)
                flush()
                waiting.append((i, readers, e))
                return i, d

            key4v = key4[:, :].rearrange("p (n s k) -> p n s k", n=U, s=2)
            key8v = key8[:, :].rearrange("p (n s k) -> p n s k", n=U, s=2)
            spread_at, scored = {}, {}

            def spread(name, made):
                dst = wide_q[name][:, :].rearrange("p (n h t) -> p n h t", n=U, h=HG)
                for h in range(HG):
                    spread_at[name] = copy(dst[head(h), :, h], chunks(q[name])[head(h)], made, scored.get("u4"))

            def query_readers(name, vector):
                def readers(e, at):
                    made = tt(dve, col(q[name]), col(e), col(vector), ALU.mult, at, vT_at)
                    if name != "y8":
                        spread(name, made)
                    return made
                return readers

            i4, d4 = grown(col, fours, fours(csum), mid4, (), query_readers("y4", r))
            e = fn(col(out["ys"]), col(diff[i4]), ACT.Exp, d4, scale=-1.0)
            diff_read[i4] = e
            tt(dve, key4v[:, :, 1, 0:N], chunks(out["ys"]), chunks(k2), ALU.mult, e)
            own = tt(dve, key4v[:, :, 0, 0:N], chunks(out["ys"]), chunks(b), ALU.mult)
            yield
            grown(col, fours, fours(cprev), mid4, (),
                  query_readers("u4", kk))
            half = lambda t: t[:, 0:U * 16]
            e16 = lambda t: t[:, 0:U * 16].rearrange("p (n m t) -> p n m t", n=U, m=4)

            def prev_readers(e, at):
                dve.wait(at)
                for s, src in ((1, k2), (0, b)):
                    at = dve.did(dve.e.tensor_tensor(
                        key4v[:, :, s, N:W4].rearrange("p n (m t) -> p n m t", m=4), e16(e),
                        src[:, :].rearrange("p (n m t) -> p n m t", n=U, m=4)[:, :, :, 0:4], ALU.mult))
                return at

            yield
            grown(half, lambda t: t[:, 0:U * 16].rearrange("p (q t) -> p q t", t=4),
                  eights(csum)[:, :, 5:6].to_broadcast([P, U * 4, 4]), eights(csum)[:, :, 0:4], (), prev_readers)
            yield
            grown(col, eights, eights(csum), first8, (),
                  query_readers("y8", r))
            yield
            grown(col, eights, eights(cprev), first8, (),
                  query_readers("u8", kk))
            offset = 0
            for j in (1, 2, 3):
                n_keys = 8 * j
                view = lambda t, n_keys=n_keys: t[:, 0:U * n_keys].rearrange("p (n t) -> p n t", n=U)

                def cross_readers(e, at, offset=offset, n_keys=n_keys, view=view):
                    dve.wait(at)
                    for s, src in ((1, k2), (0, b)):
                        at = dve.did(dve.e.tensor_tensor(key8v[:, :, s, offset:offset + n_keys], view(e),
                                                         chunks(src)[:, :, 0:n_keys], ALU.mult))
                    return at

                grown(lambda t, n_keys=n_keys: t[:, 0:U * n_keys], view,
                      chunks(cprev)[:, :, n_keys:n_keys + 1].to_broadcast([P, U, n_keys]),
                      chunks(csum)[:, :, 0:n_keys], (), cross_readers)
                offset += n_keys
                yield

            flush()
            keys_at = (dve.sem, dve.n)
            e = fn(col(out["ys"]), col(csum), ACT.Exp, own)
            ys_at = tt(pool, col(out["ys"]), col(out["ys"]), col(r), ALU.mult, e)
            e = fn(col(out["us"]), col(cprev), ACT.Exp)
            us_at = tt(pool, col(out["us"]), col(out["us"]), col(kk), ALU.mult, e)
            yield
            dend = fn(decay_end[:, :].rearrange("p (n o) -> p n o", o=1), chunks(csum)[:, :, N - 1:N], ACT.Exp)

            def end_readers(e, at):
                tt(pool, col(k_end), col(e), col(k2), ALU.mult, at)
                return tt(pool, col(b_end), col(e), col(b), ALU.mult)

            grown(col, chunks, chunks(csum)[:, :, N - 1:N].to_broadcast([P, U, N]), chunks(csum), (), end_readers)
            flush()
            end_at = (pool.sem, pool.n)
            yield

            def scores(name, keys, width, group):
                bi, ps = bank()
                pe.wait(keys_at, spread_at[name])
                for m in range(4):
                    n = group * 4 + m
                    mm = pe.e.matmul(ps[:, m * 2 * width:(m + 1) * 2 * width], wide_q[name][:, n * P:(n + 1) * P],
                                     keys[:, n * 2 * width:(n + 1) * 2 * width], start=True, stop=True)
                scored[name] = pe.did(mm)
                dve.wait(scored[name])
                return bi, ps[:, 0:8 * width].rearrange("p (n k) -> p n k", k=width)

            def target(scores_of, group):
                return scores_of[:, group * 8 * N:(group + 1) * 8 * N].rearrange("p (n t) -> p n t", t=N)

            def near(name, dst, own_mask):
                m_own = wt[own_mask][:, :].rearrange("p (o t) -> p o t", o=1).to_broadcast([P, 8, N])
                m_prev = wt["prev"][:, :].rearrange("p (o m t) -> p o m t", o=1, m=4).to_broadcast([P, 8, 4, 4])
                for group in range(U // 4):
                    bi, src = scores(name, key4, W4, group)
                    d = target(dst, group)
                    own = dve.did(dve.e.copy_predicated(d, m_own, src[:, :, 0:N]))
                    dve.wait(own)
                    last_read[bi] = dve.did(dve.e.copy_predicated(
                        d.rearrange("p n (m t) -> p n m t", t=8)[:, :, :, 0:4], m_prev,
                        src[:, :, N:W4].rearrange("p n (m t) -> p n m t", m=4)))
                    yield

            def far(name, dst):
                dve.wait((dve.sem, dve.n))
                for group in range(U // 4):
                    bi, src = scores(name, key8, W8, group)
                    offset = 0
                    for j in (1, 2, 3):
                        m = wt[f"cross{j}"][:, 0:8 * j].rearrange("p (o t) -> p o t", o=1).to_broadcast([P, 8, 8 * j])
                        last_read[bi] = dve.did(dve.e.copy_predicated(
                            target(dst, group)[:, :, 0:8 * j], m, src[:, :, offset:offset + 8 * j]))
                        dve.wait(last_read[bi])
                        offset += 8 * j
                    yield

            yield from near("u4", a_u, "own_u")
            spread("y8", None)
            yield from near("y4", a_y, "own_y")
            turn(col(out["kT"]), col(k_end), end_at)
            turn(col(out["bT"]), col(b_end))
            yield from far("u8", a_u)
            aTu_at = turn(col(aT_u), col(a_u))
            yield from far("y8", a_y)
            aTy_at = turn(col(aT_y), col(a_y), spread_at["u8"])

            a_ub = a_u[:, :].rearrange("p (n s t) -> p n s t", n=U, s=2)[:, :, 0]
            aT_ub = aT_u[:, :].rearrange("p (n s t) -> p n s t", n=U, s=2)[:, :, 0]
            every = lambda m: m.rearrange("p (o t) -> p o t", o=1).to_broadcast([P, U, N])
            t0 = tt(dve, chunks(inv), a_ub, every(wt["pair_u"][:, :]), ALU.mult)
            t1 = tt(dve, chunks(invT), aT_ub, every(wt["pair_uT"][:, :]), ALU.mult, aTu_at)
            t0 = tt(dve, chunks(inv), chunks(inv), every(wt["eye"][:, :]), ALU.add, t0)
            t1 = tt(dve, chunks(invT), chunks(invT), every(wt["eye"][:, :]), ALU.add, t1)

            yield

        def back(i, got):
            base, gate, bonus_v, aT_u, aT_y, decay_end, kT, bT, vT, inv = (got[n] for n in (
                "base", "gate", "bonus_v", "aT_u", "aT_y", "decay_end", "kT", "bT", "vT", "inv"))
            invT = [got["invT"], invT1]
            aT_ub = aT_u[:, :].rearrange("p (n s t) -> p n s t", n=U, s=2)[:, :, 0]
            every = lambda m: m.rearrange("p (o t) -> p o t", o=1).to_broadcast([P, U, N])
            HU = U // 2
            half_of = lambda t, s: t[:, s * HU * N:(s + 1) * HU * N]

            def blocks_mm(s, lhsT, rhs_t, *needs):
                bi, ps = bank("back")
                pe.wait(*needs)
                for n in range(HU):
                    for h in range(HG):
                        at = blk(s * HU + n)
                        mm = pe.e.matmul(ps[head(h), blk(n)], lhsT[head(h), at], rhs_t[head(h), at],
                                         start=n == 0, stop=n == HU - 1, skip_group_check=True)
                return bi, ps, pe.did(mm)

            inv_at, invT_at, sub_free = [None, None], [None, None], None
            for level in range(4):
                old, new = invT[level % 2], invT[(level + 1) % 2]
                s_at = tt(dve, chunks(sub), aT_ub, every(wt["subT"][:, blk(level)]), ALU.mult, sub_free)
                p_at = [None, None]
                for s in range(2):
                    bi, ps, sub_free = blocks_mm(s, sub, inv, s_at, inv_at[s])
                    p_at[s] = last_read[bi] = copy(half_of(part, s), ps[:, 0:HU * N], sub_free)
                    yield
                for s in range(2):
                    bi, ps, done = blocks_mm(s, part, old, p_at[s], invT_at[s])
                    invT_at[s] = last_read[bi] = tt(dve, half_of(new, s), half_of(old, s), ps[:, 0:HU * N], ALU.add, done)
                    if level < 3:
                        inv_at[s] = turn(half_of(inv, s), half_of(new, s), invT_at[s])
                    yield
            solve = invT[0]

            aTu = lambda n, s: slice((n * 2 + s) * N, (n * 2 + s + 1) * N)
            HS = SU // 2
            mine = lambda t, s: t[:, s * HS * N:(s + 1) * HS * N]
            wide = lambda t: t.rearrange("p (n t) -> p n t", t=N)
            state_at, y_at = [None, None], [None, None]
            decay = decay_end[:, :].rearrange("p (n c o) -> p n c o", c=NC, o=1)
            for c in range(NC):
                units = [[(u, (s * HS + u) * NC + c, s * HS + u) for u in range(HS)] for s in range(2)]
                z_at, u_at, faded_at = [None, None], [None, None], [None, None]
                for s in range(2):
                    bi, ps = bank("back")
                    pe.wait(state_at[s])
                    for u, n, su in units[s]:
                        for h in range(HG):
                            pe.e.matmul(ps[head(h), blk(u)], aT_u[head(h), aTu(n, 1)], vT[head(h), blk(n)],
                                        start=u == 0, stop=False, skip_group_check=True)
                            mm = pe.e.matmul(ps[head(h), blk(u)], got["us"][head(h), blk(n)], state[head(h), blk(su)],
                                             start=False, stop=u == HS - 1, skip_group_check=True)
                    done = pe.did(mm)
                    z_at[s] = last_read[bi] = copy(mine(rhs, s), ps[:, 0:HS * N], done)
                    faded_at[s] = tt(pool, wide(mine(faded, s)), wide(mine(state, s)),
                                     decay[:, s * HS:(s + 1) * HS, c].to_broadcast([P, HS, N]),
                                     ALU.mult, state_at[s], sub_free)
                    yield
                for s in range(2):
                    bi, ps = bank("back")
                    pe.wait(z_at[s], invT_at[s])
                    for u, n, su in units[s]:
                        for h in range(HG):
                            mm = pe.e.matmul(ps[head(h), blk(u)], solve[head(h), blk(n)], rhs[head(h), blk(su)],
                                             start=u == 0, stop=u == HS - 1, skip_group_check=True)
                    done = pe.did(mm)
                    u_at[s] = last_read[bi] = copy(mine(corr, s), ps[:, 0:HS * N], done)
                    yield
                for s in range(2):
                    sbi, sps = bank("back")
                    pe.wait(u_at[s])
                    for u, n, su in units[s]:
                        for h in range(HG):
                            hd = head(h)
                            pe.e.matmul(sps[hd, blk(u)], bT[hd, blk(n)], corr[hd, blk(su)],
                                        start=u == 0, stop=False, skip_group_check=True)
                            mm = pe.e.matmul(sps[hd, blk(u)], kT[hd, blk(n)], vT[hd, blk(n)],
                                             start=False, stop=u == HS - 1, skip_group_check=True)
                    s_done = pe.did(mm)
                    ybi, yps = bank("back")
                    for u, n, su in units[s]:
                        for h in range(HG):
                            hd = head(h)
                            pe.e.matmul(yps[hd, blk(u)], aT_y[hd, aTu(n, 0)], corr[hd, blk(su)],
                                        start=u == 0, stop=False, skip_group_check=True)
                            pe.e.matmul(yps[hd, blk(u)], aT_y[hd, aTu(n, 1)], vT[hd, blk(n)],
                                        start=False, stop=False, skip_group_check=True)
                            mm = pe.e.matmul(yps[hd, blk(u)], got["ys"][hd, blk(n)], state[hd, blk(su)],
                                             start=False, stop=u == HS - 1, skip_group_check=True)
                    done = pe.did(mm)
                    last_read[sbi] = state_at[s] = tt(dve, mine(state, s), mine(faded, s), sps[:, 0:HS * N],
                                                      ALU.add, done, faded_at[s])
                    y_at[s] = last_read[ybi] = copy(
                        y[:, :].rearrange("p (n c t) -> p n c t", c=NC, t=N)[:, s * HS:(s + 1) * HS, c],
                        wide(yps[:, 0:HS * N]), done)
                    yield

            m_of = lambda t: t[:, :].rearrange("p (n o) -> p n o", o=1).to_broadcast([P, U, N])
            dve.wait(*y_at)
            s0 = dve.did(dve.e.tensor_reduce(mean[:, :], chunks(y), AX.X, ALU.add))
            s0 = ts(dve, mean[:, :], mean[:, :], 1.0 / N, None, ALU.mult, None, s0)
            c0 = tt(dve, chunks(y), chunks(y), m_of(mean), ALU.subtract, s0)
            s1 = fn(col(squares), col(y), ACT.Square, c0)
            dve.wait(s1)
            s2 = dve.did(dve.e.tensor_reduce(var[:, :], chunks(squares), AX.X, ALU.add))
            s2 = ts(dve, var[:, :], var[:, :], 1.0 / N, 6.4e-4, ALU.mult, ALU.add, s2)
            yield
            s4 = tt(pool, var[:, :], var[:, :], minus_half, ALU.pow, s2)
            c1 = tt(dve, chunks(y), chunks(y), m_of(var), ALU.mult, s4)
            yc = turn(col(inv), col(y), c1)
            dve.wait(yc)
            for g in range(G):
                ln_at = dve.did(dve.e.tensor_scalar(grp(mixed, g), grp(inv, g), wt["ln_w"][:, g:g + 1],
                                                    wt["ln_b"][:, g:g + 1], ALU.mult, ALU.add))
            yield
            o0 = tt(dve, col(mixed), col(mixed), col(bonus_v), ALU.add, ln_at)
            o1 = tt(dve, col(mixed), col(mixed), col(gate), ALU.mult, o0)
            bi, ps = bank("back")
            pe.wait(o1)
            for g in range(G):
                mm = pe.e.matmul(ps[:, :], grp(mixed, g), wt["output"][:, g * C:(g + 1) * C], start=g == 0, stop=g == G - 1)
            done = pe.did(mm)
            acc_at = last_read[bi] = tt(dve, col(acc), col(ps), col(base), ALU.add, done)
            sp.wait(acc_at)
            for s in range(B):
                core.dma(sp, "w_acc", tile_rows(dram["acc"], i, s), acc[s * TB:(s + 1) * TB, :])

        def together(ahead, behind=None):
            owed = 0.0
            for turn_, _ in enumerate(ahead or ()):
                owed += PACE[min(turn_ // 8, len(PACE) - 1)]
                while behind and owed >= 1.0:
                    next(behind, None)
                    owed -= 1.0
            for _ in behind or ():
                pass
            core.meet()
            for n in range(8):
                last_read[n] = None

        PACE = (0.5, 0.5, 0.3, 1.0, 0.5, 1.4, 1.2)
        tiles = T // TB
        load_rows(0)
        core.meet()
        together(front(0, handed[0], 1))
        with nc.Fori(0, tiles // 2 - 1) as pair:
            together(front(pair * 2 + 1, handed[1], pair * 2 + 2), back(pair * 2, handed[0]))
            together(front(pair * 2 + 2, handed[0], pair * 2 + 3), back(pair * 2 + 1, handed[1]))
        together(front(tiles - 1, handed[1], None), back(tiles - 2, handed[0]))
        together(None, back(tiles - 1, handed[1]))


def time_mix_inputs(d):
    chan = lambda a: np.ascontiguousarray(a.reshape(G, P).T)
    kin = lambda a: np.ascontiguousarray(
        a.T.reshape(G, P, a.shape[0]).transpose(1, 0, 2).reshape(P, -1))

    def rows(width, *parts):
        out = np.zeros((P, width), np.float32)
        for at, a in parts:
            out[at:at + a.shape[0]] = a
        return out

    low_wa, low_k = np.zeros((P, C), np.float32), np.zeros((P, C), np.float32)
    low_wa[0:64], low_wa[64:80], low_wa[96:112] = d["time_decay_w1"], d["time_aaa_w1"], d["ma_w1"]
    low_k[0:16], low_k[32:48] = d["time_kkk_w1"], d["mk_w1"]
    maa_w2 = np.zeros((4, 32, 4, C), np.float32)
    for f in range(4):
        maa_w2[f, :, f] = d["time_maa_w2"][f].T
    t, i = np.arange(P)[:, None] % N, np.arange(N)[None]
    u16 = np.arange(16)[None]
    same = lambda size: t // size == i // size
    lower = {h: same(2 * h) & (t // h == i // h + 1) for h in (1, 2, 4, 8, 16)}
    upper = {h: same(2 * h) & (t // h == i // h - 1) for h in (1, 2, 4, 8, 16)}
    f32 = lambda a: np.ascontiguousarray(a.astype(np.float32))
    i32 = lambda a: np.ascontiguousarray(a.astype(np.int32))
    hot = lambda at: f32(np.arange(P)[:, None] == at)
    one = lambda name: d[name].reshape(1, C)
    out = {
        "receptance": kin(d["receptance"]), "key_w": kin(d["key_w"]), "value": kin(d["value"]),
        "output": kin(d["output"]), "maa_w1": kin(d["time_maa_w1"]), "gate_w1": kin(d["gate_w1"]),
        "maa_w2": maa_w2.reshape(P, 4 * C), "gate_w2": np.ascontiguousarray(d["gate_w2"].T),
        "low_wa": kin(low_wa), "low_k": kin(low_k),
        "decay_w2": rows(C, (0, d["time_decay_w2"].T), (80, one("time_decay"))),
        "mk_aaa_w2": rows(C, (32, d["mk_w2"].T), (48, one("time_misc_k")),
                          (64, d["time_aaa_w2"].T), (80, one("time_aaaaa"))),
        "kkk_ma_w2": rows(C, (0, d["time_kkk_w2"].T), (96, d["ma_w2"].T), (80, one("time_misc_a"))),
        "ident": np.eye(P, dtype=np.float32),
        "head_ones": f32(np.arange(P)[:, None] // N == np.arange(P)[None] // N),
        "eye": f32(t == i), "minus_half": np.full((P, 1), -0.5, np.float32), "one_wa": hot(80), "one_k": hot(48),
        "maa_x": chan(d["time_maa_x"].reshape(C)),
        "maa": np.concatenate([chan(d["time_maa"][f].reshape(C)) for f in range(4)], 1),
        "faaaa": chan(d["time_faaaa"]), "ln_w": chan(d["ln_w"]), "ln_b": chan(d["ln_b"]),
        "restart": f32(np.tile(np.arange(G * P)[None] % N != 0, (P, 1))),
        "pair_u": f32(lower[1]), "pair_uT": f32(upper[1]),
        "subT": np.concatenate([f32(upper[h]) for h in (2, 4, 8, 16)], 1),
        "own_u": i32(same(4) & (i < t)), "own_y": i32(same(4) & (i <= t)),
        "prev": i32(t // 4 == 2 * (u16 // 4) + 1),
    }
    for j in (1, 2, 3):
        out[f"cross{j}"] = i32(np.broadcast_to(t // 8 == j, (P, 24)))
    return {"w_" + k: v for k, v in out.items()}


def experts(nc, core, dram):
    pe, dve, act, pool, sp = core.queues
    FC, KT = F // P, CAP // P
    HALF = 512
    with ExitStack() as ctx:
        def sb(name, width, dt=F32):
            return ctx.enter_context(nc.sbuf_tensor("moe_" + name, [P, width], dt))

        w1, w2 = sb("w1", G * F), sb("w2", FC * C)
        h_rows, acc_rows, result, hT = sb("h_rows", KT * C), sb("acc_rows", KT * C), sb("result", KT * C), sb("hT", G * CAP)
        hidden = [sb(f"hidden{i}", HALF) for i in range(4)]
        ident, b1_all, b1, b2 = sb("ident", P), sb("b1_all", E * FC), sb("b1", FC), sb("b2", C)
        order = sb("order", E * KT, I32)
        slots, slots_next = sb("slots", KT, I32), sb("slots_next", KT, I32)
        banks = [ctx.enter_context(nc.psum_tensor(f"moe_bank{i}", [P, 512], F32)) for i in range(8)]

        w1v = w1[:, :].rearrange("p (g f) -> p g f", g=G)
        w1_dram = lambda e: dram["w1"][bass.ds(e, 1)].rearrange("o (g p) f -> (o p) g f", p=P)
        w2_dram = lambda e: dram["w2"][bass.ds(e, 1)].rearrange("o (k p) c -> (o p) k c", p=P)
        w2v = w2[:, :].rearrange("p (k c) -> p k c", k=FC)
        tile = lambda a, t: a[:, t * C:(t + 1) * C]

        def gather(rows, source, index, counter):
            for t in range(KT):
                pool.e.indirect_dma_start(tile(rows, t), None, source,
                                          bass.IndirectOffsetOnAxis(ap=index[:, t:t + 1], axis=0)).then_inc(counter, 16)

        core.dma(sp, "const", ident[:, :], dram["ident"])
        core.dma(sp, "const", b1_all[:, :], dram["b1"])
        with nc.allow_non_contiguous_dma(reason="one token index per partition and tile, loaded once"):
            got = core.dma(sp, "const", order[:, :], dram["order"].rearrange("(t p) o -> p (t o)", p=P))
        core.dma(sp, "weights", w1v, w1_dram(0))
        core.dma(sp, "weights", w2v, w2_dram(0))
        dve.wait(got)
        got = dve.did(dve.e.tensor_copy(slots_next[:, :], order[:, 0:KT]))
        pool.wait(got)
        gather(h_rows, dram["h"], slots_next, core.got_h)
        core.pool_sees(core.got_h, KT * 16)
        core.meet()

        def expert(e, is_last):
            new_slots = dve.did(dve.e.tensor_copy(slots[:, :], order[:, bass.ds(e * KT, KT)]))
            b1_at = dve.did(dve.e.tensor_copy(b1[:, :], b1_all[:, bass.ds(e * FC, FC)]))
            b2_at = core.dma(sp, "b2", b2[:, :], dram["b2"][bass.ds(e, 1)].to_broadcast([P, C]))
            pool.wait(new_slots)
            gather(acc_rows, dram["acc"], slots, core.got_acc)

            free = [None] * 8
            for t in range(KT):
                pe.wait(free[t])
                for g in range(G):
                    turned = pe.did(pe.e.transpose(banks[t][:, g * P:(g + 1) * P],
                                                   h_rows[:, t * C + g * P:t * C + (g + 1) * P], ident[:, :]))
                dst = hT[:, :].rearrange("p (g t) -> p g t", g=G)[:, :, t * P:(t + 1) * P]
                src = banks[t][:, :].rearrange("p (g t) -> p g t", g=G)
                if t % 2:
                    dve.wait(turned)
                    free[t] = dve.did(dve.e.tensor_copy(dst, src))
                else:
                    act.wait(turned)
                    free[t] = act.did(act.e.copy(dst, src))
            hT_at = free[KT - 2], free[KT - 1]
            if not is_last:
                more = dve.did(dve.e.tensor_copy(slots_next[:, :], order[:, bass.ds(e * KT + KT, KT)]))
                pool.wait(more, turned)
                gather(h_rows, dram["h"], slots_next, core.got_h)
            core.pool_sees(core.got_acc, e * (KT * 16) + KT * 16)
            pool.wait(b2_at)
            for t in range(KT):
                biased = pool.did(pool.e.tensor_tensor(tile(acc_rows, t), tile(acc_rows, t), b2[:, :], ALU.add))

            up, down = banks[0:4], banks[4:8]
            activated, used = {}, {}
            up_free, down_free = [free[i] for i in range(4)], [free[4 + i] for i in range(4)]
            steps = [(half, k) for half in range(2) for k in range(FC)]
            drained = []

            def widen(at):
                half, k = steps[at]
                bank = up[at % 4]
                pe.wait(up_free[at % 4], *hT_at)
                for g in range(G):
                    mm = pe.e.matmul(bank[:, :], w1[:, g * F + k * P:g * F + (k + 1) * P],
                                     hT[:, g * CAP + half * HALF:g * CAP + (half + 1) * HALF],
                                     start=g == 0, stop=g == G - 1)
                act.wait(pe.did(mm), used.get(at - 4), b1_at)
                activated[at] = up_free[at % 4] = act.did(act.e.activation(
                    hidden[at % 4][:, :], bank[:, :], ACT.Gelu_apprx_tanh, bias=b1[:, k:k + 1]))

            def narrow(at):
                half, k = steps[at]
                pe.wait(activated[at])
                for t in range(4):
                    if k == 0:
                        pe.wait(down_free[t])
                    mm = pe.e.matmul(down[t][:, :], hidden[at % 4][:, t * P:(t + 1) * P], tile(w2, k),
                                     start=k == 0, stop=k == FC - 1)
                used[at] = pe.did(mm)
                if half == 1 and not is_last and k % 4 == 3:
                    sp.wait(used[at])
                    lo = k - 3
                    core.dma(sp, "weights", w1v[:, :, lo * P:(k + 1) * P], w1_dram(e + 1)[:, :, lo * P:(k + 1) * P])
                    core.dma(sp, "weights", w2v[:, lo:k + 1], w2_dram(e + 1)[:, lo:k + 1])
                if k == FC - 1:
                    dve.wait(used[at], biased)
                    for t in range(4):
                        down_free[t] = dve.did(dve.e.tensor_tensor(
                            tile(result, half * 4 + t), down[t][:, :], tile(acc_rows, half * 4 + t), ALU.add))
                        pool.wait(down_free[t])
                        pool.e.indirect_dma_start(
                            dram["out"], bass.IndirectOffsetOnAxis(ap=slots[:, half * 4 + t:half * 4 + t + 1], axis=0),
                            tile(result, half * 4 + t), None).then_inc(core.stored, 16)

            widen(0)
            for at in range(len(steps)):
                if at + 1 < len(steps):
                    widen(at + 1)
                narrow(at)
            core.pool_sees(core.stored, e * (KT * 16) + KT * 16)
            if not is_last:
                core.pool_sees(core.got_h, e * (KT * 16) + 2 * KT * 16)
            core.meet()

        with nc.Fori(0, E - 1) as e:
            expert(e, False)
        expert(E - 1, True)


def mixer_with_experts(nc, dram):
    with ExitStack() as ctx:
        core = Core(nc, ctx)
        norm_and_scores(nc, core, dram)
        route(nc, core, dram)
        time_mix(nc, core, dram)
        experts(nc, core, dram)


def kernel(**inputs):
    import concourse.bacc as bacc
    from concourse.bass_utils import run_bass_kernel_spmd

    attn = {k[len("L0_attn_"):]: np.asarray(v) for k, v in inputs.items() if k.startswith("L0_attn_")}
    ffn = {k[len("L0_ffn_"):]: np.asarray(v) for k, v in inputs.items() if k.startswith("L0_ffn_")}
    arrays = {
        "x": attn["x"].reshape(NT, C),
        "ln_g": ffn["ln_g"].reshape(1, C), "ln_b": ffn["ln_b"].reshape(1, C),
        "centT": ffn["centroids"].T.reshape(G, P, E).transpose(1, 0, 2),
        "w1": ffn["w1"], "w2": ffn["w2"], "b2": ffn["b2"],
        "b1": ffn["b1"].reshape(E * F // P, P).T,
        "ident": np.eye(P, dtype=np.float32), "ones": np.ones((P, P), np.float32),
        "before": np.triu(np.ones((P, P), np.float32), 1),
        "steps15": np.tile(np.arange(1, 16, dtype=np.float32), (P, 1)),
        **time_mix_inputs(attn),
    }
    arrays = {k: np.ascontiguousarray(a) for k, a in arrays.items()}
    nc = bacc.Bacc("TRN2", target_bir_lowering=False, num_devices=1)
    dram = {k: nc.dram_tensor("in_" + k, a.shape, mybir.dt.from_np(a.dtype), kind="ExternalInput").ap()
            for k, a in arrays.items()}
    for name, shape, dt in (("xn", (NT, C), F32), ("h", (NT, C), F32), ("scores", (NT, E), F32),
                            ("order", (NT, 1), I32), ("acc", (NT, C), F32)):
        dram[name] = nc.dram_tensor("mid_" + name, shape, dt, kind="Internal").ap()
    dram["out"] = nc.dram_tensor("out", (NT, C), F32, kind="ExternalOutput").ap()
    mixer_with_experts(nc, dram)
    r = run_bass_kernel_spmd(nc, [{"in_" + k: a for k, a in arrays.items()}], core_ids=[0])
    return r.results[0]["out"].reshape(B, T, C)
```
